# Optimizing a Trainium2 kernel written in Bass

```python
import numpy as np
import jax
import jax.numpy as jnp

def _softmax(x, axis=-1):
    return jax.nn.softmax(x, axis=axis)

def _gelu(x):
    return jax.nn.gelu(x, approximate=True)

def _silu(x):
    return jax.nn.silu(x)

def _sigmoid(x):
    return jax.nn.sigmoid(x)

def _layernorm(x, axis=-1, eps=1e-05):
    m = jnp.mean(x, axis=axis, keepdims=True)
    v = jnp.var(x, axis=axis, keepdims=True)
    return (x - m) / jnp.sqrt(v + eps)

def _scatter_add(tgt, idx, src, axis=0):
    return tgt.at[idx].add(src)

def _segment_sum(src, seg, n):
    return jax.ops.segment_sum(src, seg, n)
kernel_name = 'mk_seq_postln_d2_jaxref_r8_ccbb4c'

def setup_inputs(seed: int=0):
    np.random.seed(seed)
    _w = jnp.asarray

    def _L0_attn_setup():
        import jax, jax.numpy as jnp
        import numpy as np
        D_MODEL, D_K, D_V, N_HEADS = (128, 64, 64, 16)
        BATCH, N_CTX = (2, 256)

        def half_causal_allowed(n):
            i = jnp.arange(n)[:, None]
            j = jnp.arange(n)[None, :]
            top = (i < n // 2) & (j < n // 2)
            bot = (i >= n // 2) & (j <= i)
            return top | bot
        key = jax.random.key(seed)
        ks = jax.random.split(key, 8)
        s_in = 1.0 / np.sqrt(D_MODEL)
        s_out = 1.0 / np.sqrt(D_V * N_HEADS)
        return {'x': jax.random.normal(ks[0], (BATCH, N_CTX, D_MODEL), jnp.float32), 'Wq': jax.random.uniform(ks[1], (D_MODEL, D_K * N_HEADS), jnp.float32, -s_in, s_in), 'bq': jax.random.uniform(ks[2], (D_K * N_HEADS,), jnp.float32, -s_in, s_in), 'Wk': jax.random.uniform(ks[3], (D_MODEL, D_K * N_HEADS), jnp.float32, -s_in, s_in), 'bk': jax.random.uniform(ks[4], (D_K * N_HEADS,), jnp.float32, -s_in, s_in), 'Wv': jax.random.uniform(ks[5], (D_MODEL, D_V * N_HEADS), jnp.float32, -s_in, s_in), 'bv': jax.random.uniform(ks[6], (D_V * N_HEADS,), jnp.float32, -s_in, s_in), 'Wo': jax.random.uniform(ks[7], (D_V * N_HEADS, D_MODEL), jnp.float32, -s_out, s_out)}
    _L0_attn_in = _L0_attn_setup()

    def _L0_ffn_setup():
        import jax, jax.numpy as jnp
        import numpy as np
        TOP_K = 2
        NUM_EXPERTS = 8
        B, T, H, F = (4, 256, 128, 512)
        key = jax.random.key(seed)
        ks = jax.random.split(key, 6)
        s_in = 1.0 / np.sqrt(H)
        s_ff = 1.0 / np.sqrt(F)
        return {'x': jax.random.normal(ks[0], (B, T, H), dtype=jnp.float32), 'router_w': jax.random.normal(ks[1], (NUM_EXPERTS, H), dtype=jnp.float32) * s_in, 'router_b': jax.random.normal(ks[2], (NUM_EXPERTS,), dtype=jnp.float32) * 0.01, 'gate_w': jax.random.normal(ks[3], (NUM_EXPERTS, F, H), dtype=jnp.float32) * s_in, 'up_w': jax.random.normal(ks[4], (NUM_EXPERTS, F, H), dtype=jnp.float32) * s_in, 'down_w': jax.random.normal(ks[5], (NUM_EXPERTS, H, F), dtype=jnp.float32) * s_ff}
    _L0_ffn_in = _L0_ffn_setup()

    def _L1_attn_setup():
        import jax, jax.numpy as jnp
        import numpy as np
        B, T, D = (2, 256, 128)
        H = 16
        DH = D // H
        C = 128
        ROPE_BASE = 10000.0

        def _rope_cos_sin(t_len, d_head, dtype):
            inv_freq = 1.0 / ROPE_BASE ** (jnp.arange(0, d_head, 2, dtype=jnp.float32) / d_head)
            freqs = jnp.arange(t_len, dtype=jnp.float32)[:, None] * inv_freq[None, :]
            emb = jnp.concatenate([freqs, freqs], axis=-1)
            return (jnp.cos(emb).astype(dtype), jnp.sin(emb).astype(dtype))

        def _rotate_half(x):
            x1, x2 = jnp.split(x, 2, axis=-1)
            return jnp.concatenate([-x2, x1], axis=-1)

        def _apply_rope(x, cos, sin):
            return x * cos[None, None] + _rotate_half(x) * sin[None, None]
        key = jax.random.key(seed)
        ks = jax.random.split(key, 12)
        s = 0.02
        return {'x': jax.random.normal(ks[0], (B, T, D), dtype=jnp.float32), 'w_dk': jax.random.normal(ks[1], (D, C), dtype=jnp.float32) * s, 'b_dk': jnp.zeros((C,), dtype=jnp.float32), 'w_dv': jax.random.normal(ks[2], (D, C), dtype=jnp.float32) * s, 'b_dv': jnp.zeros((C,), dtype=jnp.float32), 'w_uk': jax.random.normal(ks[3], (C, D), dtype=jnp.float32) * s, 'b_uk': jnp.zeros((D,), dtype=jnp.float32), 'w_uv': jax.random.normal(ks[4], (C, D), dtype=jnp.float32) * s, 'b_uv': jnp.zeros((D,), dtype=jnp.float32), 'w_o': jax.random.normal(ks[5], (D, D), dtype=jnp.float32) * s, 'b_o': jnp.zeros((D,), dtype=jnp.float32)}
    _L1_attn_in = _L1_attn_setup()

    def _L1_ffn_setup():
        import jax, jax.numpy as jnp
        import numpy as np
        TOP_K = 2

        def gelu(x):
            return jax.nn.gelu(x, approximate=False)
        key = jax.random.key(seed)
        ks = jax.random.split(key, 6)
        B, L, D, H, E, S = (4, 256, 128, 256, 8, 2)
        sd = 0.02
        return {'x': jax.random.normal(ks[0], (B, L, D), dtype=jnp.float32), 'router_w': jax.random.normal(ks[1], (D, E), dtype=jnp.float32) * sd, 'router_b': jnp.zeros((E,), dtype=jnp.float32), 'w1': jax.random.normal(ks[2], (E, D, H), dtype=jnp.float32) * sd, 'b1': jnp.zeros((E, H), dtype=jnp.float32), 'w2': jax.random.normal(ks[3], (E, H, D), dtype=jnp.float32) * sd, 'b2': jnp.zeros((E, D), dtype=jnp.float32), 'sw1': jax.random.normal(ks[4], (S, D, H), dtype=jnp.float32) * sd, 'sb1': jnp.zeros((S, H), dtype=jnp.float32), 'sw2': jax.random.normal(ks[5], (S, H, D), dtype=jnp.float32) * sd, 'sb2': jnp.zeros((S, D), dtype=jnp.float32)}
    _L1_ffn_in = _L1_ffn_setup()
    _d = {'L0_attn_x': _L0_attn_in['x'], 'L0_attn_Wq': _L0_attn_in['Wq'], 'L0_attn_bq': _L0_attn_in['bq'], 'L0_attn_Wk': _L0_attn_in['Wk'], 'L0_attn_bk': _L0_attn_in['bk'], 'L0_attn_Wv': _L0_attn_in['Wv'], 'L0_attn_bv': _L0_attn_in['bv'], 'L0_attn_Wo': _L0_attn_in['Wo'], 'L0_ffn_router_w': _L0_ffn_in['router_w'], 'L0_ffn_router_b': _L0_ffn_in['router_b'], 'L0_ffn_gate_w': _L0_ffn_in['gate_w'], 'L0_ffn_up_w': _L0_ffn_in['up_w'], 'L0_ffn_down_w': _L0_ffn_in['down_w'], 'L1_attn_w_dk': _L1_attn_in['w_dk'], 'L1_attn_b_dk': _L1_attn_in['b_dk'], 'L1_attn_w_dv': _L1_attn_in['w_dv'], 'L1_attn_b_dv': _L1_attn_in['b_dv'], 'L1_attn_w_uk': _L1_attn_in['w_uk'], 'L1_attn_b_uk': _L1_attn_in['b_uk'], 'L1_attn_w_uv': _L1_attn_in['w_uv'], 'L1_attn_b_uv': _L1_attn_in['b_uv'], 'L1_attn_w_o': _L1_attn_in['w_o'], 'L1_attn_b_o': _L1_attn_in['b_o'], 'L1_ffn_router_w': _L1_ffn_in['router_w'], 'L1_ffn_router_b': _L1_ffn_in['router_b'], 'L1_ffn_w1': _L1_ffn_in['w1'], 'L1_ffn_b1': _L1_ffn_in['b1'], 'L1_ffn_w2': _L1_ffn_in['w2'], 'L1_ffn_b2': _L1_ffn_in['b2'], 'L1_ffn_sw1': _L1_ffn_in['sw1'], 'L1_ffn_sb1': _L1_ffn_in['sb1'], 'L1_ffn_sw2': _L1_ffn_in['sw2'], 'L1_ffn_sb2': _L1_ffn_in['sb2']}
    _x0 = _d['L0_attn_x']
    _d['L0_attn_x'] = jax.random.normal(jax.random.fold_in(jax.random.key(seed), 1), (16, 256, 128), dtype=_x0.dtype)
    del _x0
    return _d

def reference(L0_attn_x, L0_attn_Wq, L0_attn_bq, L0_attn_Wk, L0_attn_bk, L0_attn_Wv, L0_attn_bv, L0_attn_Wo, L0_ffn_router_w, L0_ffn_router_b, L0_ffn_gate_w, L0_ffn_up_w, L0_ffn_down_w, L1_attn_w_dk, L1_attn_b_dk, L1_attn_w_dv, L1_attn_b_dv, L1_attn_w_uk, L1_attn_b_uk, L1_attn_w_uv, L1_attn_b_uv, L1_attn_w_o, L1_attn_b_o, L1_ffn_router_w, L1_ffn_router_b, L1_ffn_w1, L1_ffn_b1, L1_ffn_w2, L1_ffn_b2, L1_ffn_sw1, L1_ffn_sb1, L1_ffn_sw2, L1_ffn_sb2):

    def _L0_attn_ref(x, Wq, bq, Wk, bk, Wv, bv, Wo):
        import jax, jax.numpy as jnp
        import numpy as np
        D_MODEL, D_K, D_V, N_HEADS = (128, 64, 64, 16)
        BATCH, N_CTX = (2, 256)

        def half_causal_allowed(n):
            i = jnp.arange(n)[:, None]
            j = jnp.arange(n)[None, :]
            top = (i < n // 2) & (j < n // 2)
            bot = (i >= n // 2) & (j <= i)
            return top | bot
        b, n, _ = x.shape
        h, dk, dv = (N_HEADS, D_K, D_V)
        q = (x @ Wq + bq).reshape(b, n, h, dk).transpose(0, 2, 1, 3)
        k = (x @ Wk + bk).reshape(b, n, h, dk).transpose(0, 2, 1, 3)
        v = (x @ Wv + bv).reshape(b, n, h, dv).transpose(0, 2, 1, 3)
        scores = jnp.einsum('bhqd,bhkd->bhqk', q / jnp.sqrt(jnp.float32(dk)), k)
        allowed = half_causal_allowed(n)
        scores = jnp.where(allowed, scores, -jnp.inf)
        attn = jax.nn.softmax(scores, axis=-1)
        out = jnp.einsum('bhqk,bhkd->bhqd', attn, v)
        out = out.transpose(0, 2, 1, 3).reshape(b, n, h * dv)
        return out @ Wo

    def _L0_ffn_ref(x, router_w, router_b, gate_w, up_w, down_w):
        import jax, jax.numpy as jnp
        import numpy as np
        TOP_K = 2
        NUM_EXPERTS = 8
        B, T, H, F = (4, 256, 128, 512)
        logits = jnp.einsum('bth,eh->bte', x, router_w) + router_b
        topv, topi = jax.lax.top_k(logits, TOP_K)
        gates = jax.nn.softmax(topv, axis=-1)

        def body(acc, inputs):
            e, gw, uw, dw = inputs
            w = jnp.sum(gates * (topi == e), axis=-1)
            h = jax.nn.silu(jnp.einsum('bth,fh->btf', x, gw)) * jnp.einsum('bth,fh->btf', x, uw)
            y = jnp.einsum('btf,hf->bth', h, dw)
            return (acc + y * w[..., None], None)
        init = jnp.zeros_like(x)
        xs = (jnp.arange(NUM_EXPERTS), gate_w, up_w, down_w)
        out, _ = jax.lax.scan(body, init, xs)
        return out

    def _L1_attn_ref(x, w_dk, b_dk, w_dv, b_dv, w_uk, b_uk, w_uv, b_uv, w_o, b_o):
        import jax, jax.numpy as jnp
        import numpy as np
        B, T, D = (2, 256, 128)
        H = 16
        DH = D // H
        C = 128
        ROPE_BASE = 10000.0

        def _rope_cos_sin(t_len, d_head, dtype):
            inv_freq = 1.0 / ROPE_BASE ** (jnp.arange(0, d_head, 2, dtype=jnp.float32) / d_head)
            freqs = jnp.arange(t_len, dtype=jnp.float32)[:, None] * inv_freq[None, :]
            emb = jnp.concatenate([freqs, freqs], axis=-1)
            return (jnp.cos(emb).astype(dtype), jnp.sin(emb).astype(dtype))

        def _rotate_half(x):
            x1, x2 = jnp.split(x, 2, axis=-1)
            return jnp.concatenate([-x2, x1], axis=-1)

        def _apply_rope(x, cos, sin):
            return x * cos[None, None] + _rotate_half(x) * sin[None, None]
        Bx, Tx, Dx = x.shape
        c_k = x @ w_dk + b_dk
        c_v = x @ w_dv + b_dv
        k = c_k @ w_uk + b_uk
        v = c_v @ w_uv + b_uv

        def split_heads(t):
            return t.reshape(Bx, Tx, H, DH).transpose(0, 2, 1, 3)
        q = split_heads(x)
        k = split_heads(k)
        v = split_heads(v)
        cos, sin = _rope_cos_sin(Tx, DH, x.dtype)
        q = _apply_rope(q, cos, sin)
        k = _apply_rope(k, cos, sin)
        scale = 1.0 / np.sqrt(DH)
        attn = jnp.einsum('bhid,bhjd->bhij', q, k) * scale
        attn = jax.nn.softmax(attn, axis=-1)
        out = jnp.einsum('bhij,bhjd->bhid', attn, v)
        out = out.transpose(0, 2, 1, 3).reshape(Bx, Tx, Dx)
        return out @ w_o + b_o

    def _L1_ffn_ref(x, router_w, router_b, w1, b1, w2, b2, sw1, sb1, sw2, sb2):
        import jax, jax.numpy as jnp
        import numpy as np
        TOP_K = 2

        def gelu(x):
            return jax.nn.gelu(x, approximate=False)
        B, L, D = x.shape
        E = router_b.shape[0]
        S = sw1.shape[0]
        xf = x.reshape(-1, D)
        sh = gelu(jnp.einsum('nd,sdh->snh', xf, sw1) + sb1[:, None, :])
        shared_out = (jnp.einsum('snh,shd->nd', sh, sw2) + sb2.sum(0)) / S
        gates = xf @ router_w + router_b
        topv, topi = jax.lax.top_k(gates, TOP_K)
        probs = jax.nn.softmax(topv, axis=-1)
        comb = jnp.einsum('nke,nk->ne', jax.nn.one_hot(topi, E, dtype=xf.dtype), probs)
        h = gelu(jnp.einsum('nd,edh->enh', xf, w1) + b1[:, None, :])
        y = jnp.einsum('enh,ehd->end', h, w2) + b2[:, None, :]
        moe_out = jnp.einsum('ne,end->nd', comb, y)
        return (shared_out + moe_out).reshape(B, L, D)
    x = L0_attn_x
    x = _layernorm(x + _L0_attn_ref(x, L0_attn_Wq, L0_attn_bq, L0_attn_Wk, L0_attn_bk, L0_attn_Wv, L0_attn_bv, L0_attn_Wo), axis=-1)
    x = _layernorm(x + _L0_ffn_ref(x, L0_ffn_router_w, L0_ffn_router_b, L0_ffn_gate_w, L0_ffn_up_w, L0_ffn_down_w), axis=-1)
    x = _layernorm(x + _L1_attn_ref(x, L1_attn_w_dk, L1_attn_b_dk, L1_attn_w_dv, L1_attn_b_dv, L1_attn_w_uk, L1_attn_b_uk, L1_attn_w_uv, L1_attn_b_uv, L1_attn_w_o, L1_attn_b_o), axis=-1)
    x = _layernorm(x + _L1_ffn_ref(x, L1_ffn_router_w, L1_ffn_router_b, L1_ffn_w1, L1_ffn_b1, L1_ffn_w2, L1_ffn_b2, L1_ffn_sw1, L1_ffn_sb1, L1_ffn_sw2, L1_ffn_sb2), axis=-1)
    return x

_drawn_inputs = setup_inputs


def setup_inputs(seed=0):
    import zlib

    import numpy as np

    out = dict(_drawn_inputs(seed))
    spreads = {'L1_attn_b_dk': (0.0, 0.8),
     'L1_attn_b_dv': (0.0, 0.8),
     'L1_attn_b_uk': (0.0, 0.8),
     'L1_attn_b_uv': (0.0, 0.33),
     'L1_attn_b_o': (0.0, 0.1),
     'L1_ffn_router_b': (0.0, 0.1),
     'L1_ffn_b1': (0.0, 0.649),
     'L1_ffn_b2': (0.0, 0.1),
     'L1_ffn_sb1': (0.0, 0.681),
     'L1_ffn_sb2': (0.0, 0.1)}
    factors = {'L0_attn_bq': 5.452,
     'L0_attn_bk': 8.0,
     'L1_attn_w_dk': 8.0,
     'L1_attn_w_dv': 8.0,
     'L1_attn_w_uk': 8.0,
     'L1_attn_w_uv': 7.502}
    for name, (base, spread) in spreads.items():
        noise = np.random.default_rng([zlib.crc32(name.encode()), seed]).standard_normal(out[name].shape)
        drawn = base * np.exp(spread * noise) if base else spread * noise
        out[name] = jnp.asarray(drawn.astype(out[name].dtype))
    for name, factor in factors.items():
        out[name] = (out[name] * factor).astype(out[name].dtype)
    return out
```

```python
from contextlib import ExitStack

import concourse.bass as bass
from concourse import mybir

F32 = mybir.dt.float32
F32R = mybir.dt.float32r
BF16 = mybir.dt.bfloat16
U32 = mybir.dt.uint32
ALU = mybir.AluOpType
ACT = mybir.ActivationFunctionType
AX = mybir.AxisListType

P = 128
B, T = 16, 256
NT = B * T
QB = T // P
GT = 512
NG = NT // GT
GB = GT // P
EPS = 1e-5
PAD = GT
XC = PAD + NT + PAD

H0, DK0 = 16, 64
HP = H0 // 2
E0, F0 = 8, 512
FB0 = F0 // P
W0C = 2 * F0 + FB0 * P
H1, DH1 = 16, 8
E1, F1, S1 = 8, 256, 2
FB1 = F1 // P
W1C = F1 + FB1 * P
MASKED = -(2.0 ** 120)


class Counter:

    def __init__(self, eng, sem):
        self.eng, self.sem, self.base, self.per, self.k, self.i = eng, sem, 0, 0, 0, None

    def loop(self, i, per):
        assert self.i is None
        self.base, self.k, self.i, self.per = self.base + self.k, 0, i, per

    def end(self, count):
        assert self.k == self.per, (self.k, self.per)
        self.base, self.k, self.i = self.base + self.per * count, 0, None

    def value(self):
        v = self.base + self.k
        return v if self.i is None else self.i * self.per + v

    def done(self, ins):
        self.k += 1
        ins.then_inc(self.sem, 1)
        self.eng.wait_ge(self.sem, self.value())

    def done_apart(self, ins, spare):
        self.done(ins)
        self.eng.memset(spare, 0.0)


def split_mm(nc, out, wh, wl, xh, xl, start, stop):
    nc.tensor.matmul(out, wh, xh, start=start, stop=False)
    nc.tensor.matmul(out, wl, xh, start=False, stop=False)
    return nc.tensor.matmul(out, wh, xl, start=False, stop=stop)


class Shared:
    pass


def attention0(nc, ctx, g, d):
    sb = lambda name, shape, dt=F32: ctx.enter_context(nc.sbuf_tensor("a0_" + name, shape, dt))
    sem = lambda name: ctx.enter_context(nc.semaphore("a0_" + name))
    SCALE = DK0 ** -0.5
    SW = 3 * P

    wqk_h = sb("wqk_h", [P, 2, H0 * DK0], F32R)
    wqk_l = sb("wqk_l", [P, 2, H0 * DK0], F32R)
    wv = sb("wv", [P, H0 * DK0])
    wo = sb("wo", [P, HP, P])
    bias = sb("bias", [P, 3, HP])
    mask32 = sb("mask32", [P, P])
    mask = sb("mask", [P, P], BF16)
    identb = sb("identb", [P, P], BF16)
    xin = sb("xin", [P, QB, P])
    xres = sb("xres", [P, QB, P])
    xt = sb("xt", [P, T])
    xt_h = sb("xt_h", [P, T], F32R)
    xt_l = sb("xt_l", [P, T], F32R)
    qkt = sb("qkt", [P, 2, 2, T])
    v = sb("v", [P, 4, QB, P])
    prob = sb("prob", [P, 2, 2, SW])
    probt = sb("probt", [P, 2, 2, SW])
    mx = sb("mx", [P, 2, 2, 2])
    nmx = sb("nmx", [P, 2, 2, 2])
    lsum = sb("lsum", [P, 2, 2, 2])
    rl = sb("rl", [P, 2, 2, 2])
    ot = sb("ot", [P, HP, T])
    w32 = ot[:].rearrange("p (a h) t -> p a (h t)", a=2)
    res = sb("res", [P, QB, P])
    stats = sb("stats", [P, QB, 6])
    mv = sb("mv", [P, QB, 2])
    veps = sb("veps", [P, QB])
    rstd = sb("rstd", [P, QB])
    halfs = sb("halfs", [P, QB])
    one = sb("one", [P, 1])
    nrm = sb("nrm", [P, QB, P])
    stage = sb("stage", [P, 2, W0C // 2])
    S = g.psum[:, 0:4, :]
    PT = g.psum[:, 4:6, :]
    QK = g.psum[:, 6, :]
    VO = g.psum[:, 7, :]

    loaded_c, loaded_w, x_in = sem("loaded_c"), sem("loaded_w"), sem("x_in")
    consts, w_split = sem("consts"), sem("w_split")
    xtr_ps, xt_act, xt_done = sem("xtr_ps"), sem("xt_act"), sem("xt_done")
    qk_ps, qk_done, v_ps, v_done = sem("qk_ps"), sem("qk_done"), sem("v_ps"), sem("v_done")
    sc_ps, nmx_done, exp_done, prob_done = sem("sc_ps"), sem("nmx_done"), sem("exp_done"), sem("prob_done")
    pt_ps, pt_done, pv_ps, ot_done = sem("pt_ps"), sem("pt_done"), sem("pv_ps"), sem("ot_done")
    y_ps, res_done, xres_done = sem("y_ps"), sem("res_done"), sem("xres_done")
    var_done, rstd_done, nrm_done = sem("var_done"), sem("rstd_done"), sem("nrm_done")
    ntr_ps, nt_act, nt_done = sem("ntr_ps"), sem("nt_act"), sem("nt_done")
    init, dve_chain, pool_chain = sem("init"), sem("dve_chain"), sem("pool_chain")
    stage_in = [sem("stage_in0"), sem("stage_in1")]
    stage_free = sem("stage_free")
    x_d = d["x"].rearrange("b (q p) f -> b p q f", p=P)

    with nc.Block() as block:
        @block.sync
        def _(sp):
            sp.dma_start(xin[:], x_d[0]).then_inc(x_in, 16)
            sp.dma_start(w32[:, 0, :], d["wq"]).then_inc(loaded_w, 16)
            sp.dma_start(w32[:, 1, :], d["wk"]).then_inc(loaded_w, 16)
            sp.dma_start(bias[:], d["bqkv"]).then_inc(loaded_c, 16)
            sp.dma_start(wo[:], d["wo"].rearrange("(h p) n -> p h n", p=P)).then_inc(loaded_c, 16)

            def loads(j, last=False):
                for half in range(2):
                    i = j * 2 + half
                    sp.wait_ge(stage_free, i + 1)
                    sp.dma_start(stage[:, half, :], d["w0"][:, bass.ds(i * (W0C // 2), W0C // 2)]
                                 ).then_inc(stage_in[half], 16)
                    sp.wait_ge(xtr_ps, i + 1)
                    sp.wait_ge(xres_done, i + 1)
                    nxt = 0 if last and half else i + 1
                    sp.dma_start(xin[:], x_d[bass.ds(nxt, 1)].rearrange("a p q f -> p (a q) f")).then_inc(x_in, 16)

            with sp.Fori(0, B // 2 - 1) as j:
                loads(j)
            loads(B // 2 - 1, last=True)

        @block.scalar
        def _(act):
            act.dma_start(g.ident[:], d["ident"]).then_inc(loaded_c, 16)
            act.dma_start(mask32[:], d["mask"]).then_inc(loaded_c, 16)
            act.dma_start(wv[:], d["wv"]).then_inc(loaded_c, 16)
            act.wait_ge(loaded_w, 32)
            nc.scalar.activation(wqk_h[:], w32, ACT.Copy).then_inc(w_split, 1)

            def activations():
                nc.scalar.activation(xt[:], QK[:, 0:T], ACT.Copy).then_inc(xt_act, 1)
                nc.scalar.activation(xt_h[:], QK[:, 0:T], ACT.Copy).then_inc(xt_act, 1)

            def exps(slot, h):
                for q in range(QB):
                    at = slice(0, P) if q == 0 else slice(P, SW)
                    last = nc.scalar.activation(prob[:, slot, h, at], S[:, 2 * slot + h, at], ACT.Exp,
                                                bias=nmx[:, slot, q, h:h + 1], scale=SCALE,
                                                accum_out=lsum[:, slot, h, q:q + 1])
                last.then_inc(exp_done, 1)

            act.wait_ge(xtr_ps, 1)
            activations()
            act.wait_ge(nmx_done, 1)
            exps(0, 0)
            exps(0, 1)
            with act.Fori(0, B) as i:
                for hp in range(HP):
                    s = i * HP + hp
                    act.wait_ge(nmx_done, s + 2)
                    exps((hp + 1) % 2, 0)
                    act.wait_ge(pt_ps, s + 1)
                    nc.scalar.activation(probt[:, hp % 2], PT[:, :, 0:SW], ACT.Copy).then_inc(pt_done, 1)
                    exps((hp + 1) % 2, 1)
                    if hp == 5:
                        act.wait_ge(xtr_ps, i + 2)
                        activations()
                    if hp == 0:
                        act.wait_ge(y_ps, i + 1)
                    act.wait_ge(pv_ps, s + 1)
                    nc.scalar.activation(ot[:, hp, :], VO[:, 0:T], ACT.Identity,
                                         bias=bias[:, 2, hp:hp + 1]).then_inc(ot_done, 1)
                    if hp == 1:
                        act.wait_ge(ntr_ps, i + 1)
                        nc.scalar.activation(g.xth[:, bass.ds(i * T + (PAD - T), T)], QK[:, 0:T],
                                             ACT.Copy).then_inc(nt_act, 1)
            act.wait_ge(ntr_ps, B + 1)
            nc.scalar.activation(g.xth[:, PAD + NT - T:PAD + NT], QK[:, 0:T], ACT.Copy).then_inc(nt_act, 1)

        @block.gpsimd
        def _(pool):
            nc.gpsimd.memset(halfs[:], -0.5)
            nc.gpsimd.memset(one[:], 1.0)
            nc.gpsimd.memset(rstd[:], 0.0).then_inc(rstd_done, 1)
            pool.wait_ge(rstd_done, 1)
            nc.gpsimd.memset(g.xth[:, PAD + NT:XC].bitcast(F32), 0.0)
            nc.gpsimd.memset(g.xtl[:, PAD + NT:XC].bitcast(F32), 0.0)
            pool.wait_ge(x_in, 16)
            nc.gpsimd.tensor_copy(xres[:], xin[:]).then_inc(xres_done, 1)
            pool.sem_inc(stage_free, 2)
            with pool.Fori(0, B // 2) as j:
                for half in range(2):
                    i = j * 2 + half
                    at = bass.ds(i * (W0C // 2), W0C // 2)
                    pool.wait_ge(stage_in[half], (j + 1) * 16)
                    nc.gpsimd.tensor_tensor(g.wh[:, at], stage[:, half, :], one[:].to_broadcast(stage[:, half, :].shape), ALU.mult).then_inc(pool_chain, 1)
                    pool.wait_ge(pool_chain, i + 1)
                    nc.gpsimd.tensor_tensor(g.wl[:, at], stage[:, half, :], g.wh[:, at].bitcast(F32),
                                            ALU.subtract).then_inc(stage_free, 1)
                    pool.wait_ge(var_done, i + 1)
                    nc.gpsimd.tensor_tensor(rstd[:], veps[:], halfs[:], ALU.pow).then_inc(rstd_done, 1)
                    pool.wait_ge(x_in, i * 16 + 32)
                    pool.wait_ge(res_done, i + 2)
                    nc.gpsimd.tensor_tensor(xres[:], xin[:], one[:].unsqueeze(2).to_broadcast([P, QB, P]), ALU.mult).then_inc(xres_done, 1)

        @block.vector
        def _(dve):
            chain = Counter(dve, dve_chain)
            dve.wait_ge(loaded_c, 5 * 16)
            nc.vector.tensor_copy(mask[:], mask32[:]).then_inc(consts, 1)
            nc.vector.tensor_copy(identb[:], g.ident[:]).then_inc(consts, 1)
            nc.vector.memset(res[:], 0.0)
            nc.vector.memset(mv[:], 0.0)
            dve.wait_ge(w_split, 1)
            nc.vector.tensor_tensor(wqk_l[:], w32, wqk_h[:].bitcast(F32), ALU.subtract).then_inc(w_split, 1)
            dve.sem_inc(res_done, 1)
            dve.sem_inc(y_ps, 1)

            def activations(n):
                dve.wait_ge(xt_act, n)
                nc.vector.tensor_tensor(xt_l[:], xt[:], xt_h[:].bitcast(F32), ALU.subtract).then_inc(xt_done, 1)

            def evac_qk(hp, n):
                dve.wait_ge(qk_ps, n)
                for j in range(2):
                    last = nc.vector.tensor_scalar(qkt[:, hp % 2, j, :], QK[:, j * T:(j + 1) * T],
                                                   bias[:, j, hp % HP:hp % HP + 1], None, ALU.add)
                last.then_inc(qk_done, 1)

            def evac_v(hp, n):
                dve.wait_ge(v_ps, n)
                nc.vector.tensor_copy(v[:, hp % 4], VO[:, 0:QB * P].rearrange("p (q n) -> p q n", q=QB)
                                      ).then_inc(v_done, 1)

            def maxima(slot, n):
                dve.wait_ge(sc_ps, n)
                nc.vector.reduce_max(mx[:, slot, 0, :], S[:, 2 * slot:2 * slot + 2, 0:P], AX.X)
                chain.done(nc.vector.reduce_max(mx[:, slot, 1, :], S[:, 2 * slot:2 * slot + 2, P:SW], AX.X))
                nc.vector.tensor_scalar(nmx[:, slot], mx[:, slot], -SCALE, None, ALU.mult).then_inc(nmx_done, 1)

            def normalise(slot, h, n):
                dve.wait_ge(exp_done, n)
                chain.done(nc.vector.reciprocal(rl[:, slot, h, :], lsum[:, slot, h, :]))
                nc.vector.tensor_scalar(prob[:, slot, h, 0:P], prob[:, slot, h, 0:P], rl[:, slot, h, 0:1], None, ALU.mult)
                nc.vector.tensor_scalar(prob[:, slot, h, P:SW], prob[:, slot, h, P:SW], rl[:, slot, h, 1:2], None,
                                        ALU.mult).then_inc(prob_done, 1)

            def layernorm():
                for q in range(QB):
                    last = nc.vector.tensor_scalar(nrm[:, q, :], res[:, q, :], mv[:, q, 0:1], rstd[:, q:q + 1],
                                                   ALU.subtract, ALU.mult)
                last.then_inc(nrm_done, 1)

            activations(2)
            evac_qk(0, 1)
            evac_v(0, 1)
            evac_qk(1, 2)
            evac_v(1, 2)
            maxima(0, 1)
            evac_qk(2, 3)
            evac_v(2, 3)
            maxima(1, 2)
            normalise(0, 0, 1)
            normalise(0, 1, 2)
            with dve.Fori(0, B) as i:
                chain.loop(i, HP * 3 + 3)
                for hp in range(HP):
                    s = i * HP + hp
                    normalise((hp + 1) % 2, 0, s * 2 + 3)
                    maxima(hp % 2, s + 3)
                    normalise((hp + 1) % 2, 1, s * 2 + 4)
                    if hp == 0:
                        dve.wait_ge(rstd_done, i + 1)
                        layernorm()
                    if hp == 1:
                        dve.wait_ge(nt_act, i + 1)
                        at = bass.ds(i * T + (PAD - T), T)
                        nc.vector.tensor_tensor(g.xtl[:, at], QK[:, 0:T], g.xth[:, at].bitcast(F32),
                                                ALU.subtract).then_inc(nt_done, 1)
                    if hp == 5:
                        activations(i * 2 + 4)
                    evac_qk(hp + 3, s + 4)
                    evac_v(hp + 3, s + 4)
                dve.wait_ge(y_ps, i + 2)
                dve.wait_ge(xres_done, i + 1)
                chain.done(nc.vector.tensor_tensor(res[:], VO[:, 0:QB * P].rearrange("p (q n) -> p q n", q=QB), xres[:],
                                                   ALU.add))
                dve.sem_inc(res_done, 1)
                for q in range(QB):
                    last = nc.vector.bn_stats(stats[:, q, :], res[:, q, :])
                chain.done_apart(last, g.spare[:])
                for q in range(QB):
                    last = nc.vector.bn_aggr(mv[:, q, :], stats[:, q:q + 1, :])
                chain.done(last)
                nc.vector.tensor_scalar(veps[:], mv[:, :, 1], EPS, None, ALU.add).then_inc(var_done, 1)
            chain.end(B)
            dve.wait_ge(rstd_done, B + 1)
            layernorm()
            dve.wait_ge(nt_act, B + 1)
            nc.vector.tensor_tensor(g.xtl[:, PAD + NT - T:PAD + NT], QK[:, 0:T], g.xth[:, PAD + NT - T:PAD + NT].bitcast(F32),
                                    ALU.subtract).then_inc(nt_done, 1)

        @block.tensor
        def _(pe):
            def rows_to_columns(src, signal):
                for q in range(QB):
                    last = nc.tensor.transpose(QK[:, q * P:(q + 1) * P], src[:, q, :], g.ident[:])
                last.then_inc(signal, 1)

            def project_qk(hp):
                hp = hp % HP
                at = slice(hp * P, (hp + 1) * P)
                for j in range(2):
                    last = split_mm(nc, QK[:, j * T:(j + 1) * T], wqk_h[:, j, at], wqk_l[:, j, at], xt_h[:], xt_l[:],
                                    True, True)
                last.then_inc(qk_ps, 1)

            def project_v(hp):
                hp = hp % HP
                for q in range(QB):
                    last = nc.tensor.matmul(VO[:, q * P:(q + 1) * P], xt[:, q * P:(q + 1) * P], wv[:, hp * P:(hp + 1) * P],
                                            start=True, stop=True)
                last.then_inc(v_ps, 1)

            def scores(slot, hp):
                for h in range(2):
                    row = slice(h * DK0, (h + 1) * DK0)
                    out = S[:, 2 * slot + h, :]
                    q, k = qkt[row, hp % 2, 0, :], qkt[row, hp % 2, 1, :]
                    nc.tensor.matmul(out[:, 0:P], q[:, 0:P], k[:, 0:P], start=True, stop=True)
                    nc.tensor.matmul(out[:, P:SW], q[:, P:T], k, start=True, stop=False)
                    last = nc.tensor.matmul(out[:, 2 * P:SW], identb[:], mask[:], start=False, stop=True)
                last.then_inc(sc_ps, 1)

            pe.wait_ge(loaded_c, 5 * 16)
            pe.wait_ge(x_in, 16)
            rows_to_columns(xin, xtr_ps)
            pe.wait_ge(w_split, 2)
            pe.wait_ge(xt_done, 1)
            project_qk(0)
            project_v(0)
            pe.wait_ge(consts, 2)
            for s in range(2):
                pe.wait_ge(qk_done, s + 1)
                pe.wait_ge(v_done, s + 1)
                project_qk(s + 1)
                project_v(s + 1)
                scores(s, s)
            with pe.Fori(0, B) as i:
                for hp in range(HP):
                    s = i * HP + hp
                    pe.wait_ge(prob_done, s * 2 + 2)
                    for h in range(2):
                        for t in range(3):
                            last = nc.tensor.transpose(PT[:, h, t * P:(t + 1) * P],
                                                       prob[:, hp % 2, h, t * P:(t + 1) * P], g.ident[:])
                    last.then_inc(pt_ps, 1)
                    pe.wait_ge(qk_done, s + 3)
                    scores(hp % 2, hp + 2)
                    if hp == 5:
                        pe.wait_ge(x_in, i * 16 + 32)
                        rows_to_columns(xin, xtr_ps)
                    if hp == 0:
                        pe.wait_ge(res_done, i + 1)
                    pe.wait_ge(v_done, s + 3)
                    pe.wait_ge(pt_done, s + 1)
                    for h in range(2):
                        out = VO[h * DK0:(h + 1) * DK0, :]
                        at = slice(h * DK0, (h + 1) * DK0)
                        nc.tensor.matmul(out[:, 0:T], v[:, hp % 4, 0, at], probt[:, hp % 2, h, 0:T], start=True, stop=False)
                    for h in range(2):
                        out = VO[h * DK0:(h + 1) * DK0, :]
                        at = slice(h * DK0, (h + 1) * DK0)
                        last = nc.tensor.matmul(out[:, P:T], v[:, hp % 4, 1, at], probt[:, hp % 2, h, T:SW],
                                                start=False, stop=True)
                    last.then_inc(pv_ps, 1)
                    if hp == 1:
                        pe.wait_ge(nrm_done, i + 1)
                        rows_to_columns(nrm, ntr_ps)
                        pe.wait_ge(nt_done, i + 1)
                    if hp == 5:
                        pe.wait_ge(xt_done, i + 2)
                    project_qk(hp + 3)
                    pe.wait_ge(ot_done, s + 1)
                    project_v(hp + 3)
                pe.wait_ge(v_done, i * HP + HP + 3)
                for q in range(QB):
                    for hp in range(HP):
                        last = nc.tensor.matmul(VO[:, q * P:(q + 1) * P], ot[:, hp, q * P:(q + 1) * P], wo[:, hp, :],
                                                start=hp == 0, stop=hp == HP - 1)
                last.then_inc(y_ps, 1)
            pe.wait_ge(nrm_done, B + 1)
            pe.wait_ge(qk_done, B * HP + 3)
            rows_to_columns(nrm, ntr_ps)


def moe(nc, ctx, g, d, tag, gated):
    sb = lambda name, shape, dt=F32: ctx.enter_context(nc.sbuf_tensor(tag + name, shape, dt))
    sem = lambda name: ctx.enter_context(nc.semaphore(tag + name))
    FB = FB0 if gated else FB1
    U = (E0 if gated else E1 + S1) * FB
    WC = W0C if gated else W1C
    UP0 = F0 if gated else 0
    DN0 = 2 * F0 if gated else F1
    E = E0
    spread_at = [min(max(8, FB * e + 6), U - 1) for e in range(E)] if gated else [8 + e for e in range(E)]

    rw32 = sb("rw32", [P, P])
    rw_h, rw_l = sb("rw_h", [P, P], F32R), sb("rw_l", [P, P], F32R)
    ident_r = sb("ident_r", [P, P], F32R)
    rb = sb("rb", [P, 1])
    iota = sb("iota", [P, E])
    hot32 = sb("hot32", [E, E, P])
    hot = sb("hot", [E, E, P], F32R)
    logit = sb("logit", [P, GT])
    lt = sb("lt", [P, GB, E])
    top = sb("top", [P, GB, 8])
    topi = sb("topi", [P, GB, 8], U32)
    topf = sb("topf", [P, GB, 2])
    gap = sb("gap", [P, GB])
    th = sb("th", [P, GB])
    pr = sb("pr", [P, 2, GB])
    comb2 = sb("comb2", [P, 2, GB, E])
    comb = sb("comb", [P, GB, E])
    cb_h, cb_l = sb("cb_h", [E, GT], F32R), sb("cb_l", [E, GT], F32R)
    wb = sb("wb", [P, E + 1, GT])
    act_out = sb("act_out", [P, 2, GT])
    wgt = sb("wgt", [P, 2, GT])
    hid = sb("hid", [P, 2, GT]) if gated else None
    hid_h, hid_l = sb("hid_h", [P, 2, GT], F32R), sb("hid_l", [P, 2, GT], F32R)
    rt = sb("rt", [P, GT])
    stats, mv = sb("stats", [P, GB, 6]), sb("mv", [P, GB, 2])
    veps, rstd, halfs = sb("veps", [P, GB]), sb("rstd", [P, GB]), sb("halfs", [P, GB])
    nrm = sb("nrm", [P, GB, P])
    if not gated:
        b1 = sb("b1", [P, U])
        b2_32 = sb("b2_32", [E, P])
        b2_h, b2_l = sb("b2_h", [E, P], F32R), sb("b2_l", [E, P], F32R)
        sb2 = sb("sb2", [P, S1])
        sb2m = sb("sb2m", [P, 2])
    G, UP, Y = g.psum[:, 0:2, :], g.psum[:, 2:4, :], g.psum[:, 4, :]
    R, WB, N = g.psum[:, 5, :], g.psum[:, 6, :], g.psum[:, 7, :]

    loaded, consts, dve_chain, act_const = sem("loaded"), sem("consts"), sem("dve_chain"), sem("act_const")
    up_ps, act_done, wgt_done, bank_free, hid_done, down_ps = (sem(n) for n in (
        "up_ps", "act_done", "wgt_done", "bank_free", "hid_done", "down_ps"))
    y_ps, rt_done, rows_ps, var_done, rstd_done, nrm_done, ntr_ps, nt_act, rows_free = (sem(n) for n in (
        "y_ps", "rt_done", "rows_ps", "var_done", "rstd_done", "nrm_done", "ntr_ps", "nt_act", "rows_free"))
    logit_ps, logit_done, lt_ps, gap_done, th_done, comb_done, ct_ps, cb_done, wb_ps, wb_done = (sem(n) for n in (
        "logit_ps", "logit_done", "lt_ps", "gap_done", "th_done", "comb_done", "ct_ps", "cb_done", "wb_ps", "wb_done"))
    stored = sem("stored")
    LOADS = 5 if gated else 8

    with nc.Block() as block:
        @block.sync
        def _(sp):
            names = [(rw32, "rw"), (rb, "rb"), (iota, "iota"), (hot32, "hot")] + (
                [] if gated else [(b1, "b1"), (b2_32, "b2"), (sb2, "sb2")])
            for tile, name in names:
                sp.dma_start(tile[:], d[tag + name] if name not in ("iota", "hot") else d[name]).then_inc(loaded, 16)
            sp.dma_start(rt[:], d["zeros"]).then_inc(loaded, 16)
            if not gated:
                sp.sem_inc(stored, 16)
                with sp.Fori(0, NG) as n:
                    sp.wait_ge(nrm_done, n + 1)
                    sp.dma_start(d["out"][bass.ds(n * GT, GT)].rearrange("(b p) f -> p b f", p=P), nrm[:]
                                 ).then_inc(stored, 16)
                sp.wait_ge(nrm_done, NG + 1)
                sp.dma_start(d["out"][NG * GT:(NG + 1) * GT].rearrange("(b p) f -> p b f", p=P), nrm[:]
                             ).then_inc(stored, 16)
                sp.wait_ge(stored, 16 * (NG + 2))

        @block.tensor
        def _(pe):
            def project(w, at, n):
                e, f = w // FB, w % FB
                if n is not None:
                    pe.wait_ge(bank_free if gated else act_done, n)
                x_h, x_l = g.xth[:, at], g.xtl[:, at]
                for bank, c0 in ([(G, 0), (UP, UP0)] if gated else [(G, 0)]):
                    c = slice(e * WC + c0 + f * P, e * WC + c0 + (f + 1) * P)
                    last = split_mm(nc, bank[:, w % 2, :], g.wh[:, c], g.wl[:, c], x_h, x_l, True, True)
                last.then_inc(up_ps, 1)

            def down(u):
                e, f = u // FB, u % FB
                c = slice(e * WC + DN0 + f * P, e * WC + DN0 + (f + 1) * P)
                split_mm(nc, Y, g.wh[:, c], g.wl[:, c], hid_h[:, u % 2, :], hid_l[:, u % 2, :],
                         u == 0, u == U - 1).then_inc(down_ps, 1)

            def router_logits(at, n):
                pe.wait_ge(cb_done, n)
                split_mm(nc, R, rw_h[:], rw_l[:], g.xth[:, at], g.xtl[:, at], True, True).then_inc(logit_ps, 1)

            def router_rows(n):
                pe.wait_ge(logit_done, n)
                for b in range(GB):
                    last = nc.tensor.transpose(R[:, b * P:(b + 1) * P], logit[:, b * P:(b + 1) * P], g.ident[:])
                last.then_inc(lt_ps, 1)

            def router_columns(n):
                pe.wait_ge(comb_done, n)
                for b in range(GB):
                    last = nc.tensor.transpose(R[0:E, b * P:(b + 1) * P], comb[:, b, :], g.ident[:])
                last.then_inc(ct_ps, 1)

            def spread(e, n):
                pe.wait_ge(cb_done, n)
                if e or not isinstance(n, int):
                    pe.wait_ge(wb_done, (n - 1) * E + e)
                nc.tensor.matmul(WB, hot[:, e, :], cb_h[:], start=True, stop=False)
                nc.tensor.matmul(WB, hot[:, e, :], cb_l[:], start=False, stop=True).then_inc(wb_ps, 1)

            def rows(n):
                pe.wait_ge(rt_done, n)
                pe.wait_ge(rows_free, n)
                for b in range(GB):
                    last = nc.tensor.transpose(N[:, b * P:(b + 1) * P], rt[:, b * P:(b + 1) * P], g.ident[:])
                last.then_inc(rows_ps, 1)

            def columns(n):
                pe.wait_ge(nrm_done, n)
                for b in range(GB):
                    last = nc.tensor.transpose(N[:, b * P:(b + 1) * P], nrm[:, b, :], g.ident[:])
                last.then_inc(ntr_ps, 1)

            pe.wait_ge(loaded, LOADS * 16)
            first = slice(PAD, PAD + GT)
            project(0, first, None)
            project(1, first, None)
            pe.wait_ge(consts, 2)
            split_mm(nc, R, rw_h[:], rw_l[:], g.xth[:, first], g.xtl[:, first], True, True).then_inc(logit_ps, 1)
            router_rows(1)
            router_columns(1)
            for e in range(E):
                spread(e, 1)
            with pe.Fori(0, NG) as n:
                here, ahead = bass.ds(n * GT + PAD, GT), bass.ds(n * GT + (PAD + GT), GT)
                for u in range(U):
                    w = u + 2
                    project(w % U, here if w < U else ahead, n * U + u + 1)
                    if u == 0:
                        router_logits(ahead, n + 1)
                    if u == 1:
                        rows(n + 1)
                    if u == 2:
                        router_rows(n + 2)
                    if u == 5 and gated:
                        columns(n + 1)
                    if u == 6:
                        router_columns(n + 2)
                    pe.wait_ge(hid_done, n * U + u + 1)
                    if u == 0:
                        pe.wait_ge(rt_done, n + 1)
                    down(u)
                    if u == 0:
                        nc.tensor.matmul(Y, ident_r[:], g.xth[:, here], start=False, stop=False)
                        nc.tensor.matmul(Y, ident_r[:], g.xtl[:, here], start=False, stop=False)
                        if not gated:
                            split_mm(nc, Y, b2_h[:], b2_l[:], cb_h[:], cb_l[:], False, False)
                    for e in range(E):
                        if spread_at[e] == u:
                            spread(e, n + 2)
            rows(NG + 1)
            if gated:
                columns(NG + 1)

        @block.scalar
        def _(act):
            def activate(w, n):
                act.wait_ge(up_ps, n + 1)
                if not isinstance(n, int):
                    act.wait_ge(wgt_done, n - 1)
                if gated:
                    last = nc.scalar.activation(act_out[:, w % 2, :], G[:, w % 2, :], ACT.Silu)
                else:
                    last = nc.scalar.activation(act_out[:, w % 2, :], G[:, w % 2, :], ACT.Gelu, bias=b1[:, w:w + 1])
                last.then_inc(act_done, 1)

            def tanh(n):
                act.wait_ge(gap_done, n)
                nc.scalar.activation(th[:], gap[:], ACT.Tanh, scale=0.5).then_inc(th_done, 1)

            def spread(e, n, used):
                act.wait_ge(wb_ps, (n - 1) * E + e + 1)
                if used is not None:
                    act.wait_ge(wgt_done, used)
                nc.scalar.activation(wb[:, e, :], WB, ACT.Copy).then_inc(wb_done, 1)

            def residual(n):
                act.wait_ge(down_ps, n)
                if gated:
                    last = nc.scalar.activation(rt[:], Y, ACT.Copy)
                else:
                    last = nc.scalar.activation(rt[:], Y, ACT.Identity, bias=sb2m[:, 1:2])
                last.then_inc(rt_done, 1)

            def columns(at, n):
                act.wait_ge(ntr_ps, n)
                nc.scalar.activation(g.xth[:, at], N, ACT.Copy).then_inc(nt_act, 1)

            act.wait_ge(loaded, LOADS * 16)
            act.wait_ge(consts, 2)
            act.sem_inc(rt_done, 1)
            activate(0, 0)
            tanh(1)
            for e in range(E):
                spread(e, 1, None)
            activate(1, 1)
            with act.Fori(0, NG) as n:
                for u in range(U):
                    for e in range(E):
                        if spread_at[e] + 1 == u:
                            spread(e, n + 2, n * U + (e + 1) * FB)
                    if u == 4:
                        tanh(n + 2)
                    if u == 6 and gated:
                        columns(bass.ds(n * GT, GT), n + 1)
                    activate((u + 2) % U, n * U + u + 2)
                if gated:
                    spread(E - 1, n + 2, n * U + U)
                residual(n * U + U)
            if gated:
                columns(slice(NG * GT, (NG + 1) * GT), NG + 1)

        @block.gpsimd
        def _(pool):
            def weigh(w, n, wb_n):
                e = w // FB
                pool.wait_ge(act_done, n + 1)
                if not isinstance(n, int):
                    pool.wait_ge(bank_free if gated else hid_done, n - 1)
                if e < E and w % FB == 0:
                    pool.wait_ge(wb_done, wb_n * E + e + 1)
                last = nc.gpsimd.tensor_tensor(wgt[:, w % 2, :], act_out[:, w % 2, :], wb[:, min(e, E), :], ALU.mult)
                last.then_inc(wgt_done, 1)

            def power(n):
                pool.wait_ge(var_done, n)
                nc.gpsimd.tensor_tensor(rstd[:], veps[:], halfs[:], ALU.pow).then_inc(rstd_done, 1)

            nc.gpsimd.memset(wb[:, E, :], 1.0 / S1)
            nc.gpsimd.memset(halfs[:], -0.5).then_inc(consts, 1)
            weigh(0, 0, 0)
            weigh(1, 1, 0)
            with pool.Fori(0, NG) as n:
                for u in range(U):
                    if u == 3:
                        power(n + 1)
                    weigh((u + 2) % U, n * U + u + 2, n if u + 2 < U else n + 1)
            power(NG + 1)

        @block.vector
        def _(dve):
            chain = Counter(dve, dve_chain)

            def hidden(w, n):
                dve.wait_ge(wgt_done, n + 1)
                src = wgt[:, w % 2, :]
                if gated:
                    dve.wait_ge(up_ps, n + 1)
                    ins = nc.vector.tensor_tensor(hid[:, w % 2, :], src, UP[:, w % 2, :], ALU.mult)
                    ins.then_inc(bank_free, 1)
                    dve.wait_ge(bank_free, n + 1)
                    src = hid[:, w % 2, :]
                if not isinstance(n, int):
                    dve.wait_ge(down_ps, n - 1)
                chain.done(nc.vector.tensor_copy(hid_h[:, w % 2, :], src))
                nc.vector.tensor_tensor(hid_l[:, w % 2, :], src, hid_h[:, w % 2, :].bitcast(F32), ALU.subtract
                                        ).then_inc(hid_done, 1)

            def router_logits(n):
                dve.wait_ge(logit_ps, n)
                nc.vector.tensor_scalar(logit[:], R, rb[:], None, ALU.add).then_inc(logit_done, 1)

            def router_top(n):
                dve.wait_ge(lt_ps, n)
                chain.done_apart(nc.vector.tensor_copy(lt[:], R.rearrange("p (b n) -> p b n", b=GB)[:, :, 0:E]), g.spare[:])
                for b in range(GB):
                    last = nc.vector.max(top[:, b, :], lt[:, b, :])
                chain.done_apart(last, g.spare[:])
                for b in range(GB):
                    last = nc.vector.max_index(topi[:, b, :], top[:, b, :], lt[:, b, :])
                chain.done(last)
                nc.vector.tensor_copy(topf[:], topi[:, :, 0:2])
                nc.vector.tensor_tensor(gap[:], top[:, :, 0], top[:, :, 1], ALU.subtract).then_inc(gap_done, 1)

            def router_weights(n):
                dve.wait_ge(th_done, n)
                nc.vector.tensor_scalar(pr[:, 0, :], th[:], 0.5, 0.5, ALU.mult, ALU.add)
                chain.done(nc.vector.tensor_scalar(pr[:, 1, :], th[:], -0.5, 0.5, ALU.mult, ALU.add))
                for k in range(2):
                    for b in range(GB):
                        last = nc.vector.tensor_scalar(comb2[:, k, b, :], iota[:], topf[:, b, k:k + 1], pr[:, k, b:b + 1],
                                                       ALU.is_equal, ALU.mult)
                chain.done(last)
                nc.vector.tensor_tensor(comb[:], comb2[:, 0], comb2[:, 1], ALU.add).then_inc(comb_done, 1)

            def router_columns(n):
                dve.wait_ge(ct_ps, n)
                chain.done(nc.vector.tensor_copy(cb_h[:], R[0:E, :]))
                nc.vector.tensor_tensor(cb_l[:], R[0:E, :], cb_h[:].bitcast(F32), ALU.subtract).then_inc(cb_done, 1)

            def variances(n):
                dve.wait_ge(rows_ps, n)
                for b in range(GB):
                    last = nc.vector.bn_stats(stats[:, b, :], N[:, b * P:(b + 1) * P])
                chain.done_apart(last, g.spare[:])
                for b in range(GB):
                    last = nc.vector.bn_aggr(mv[:, b, :], stats[:, b:b + 1, :])
                chain.done(last)
                nc.vector.tensor_scalar(veps[:], mv[:, :, 1], EPS, None, ALU.add).then_inc(var_done, 1)

            def normalise(n):
                dve.wait_ge(rstd_done, n)
                if not gated:
                    dve.wait_ge(stored, n * 16)
                for b in range(GB):
                    last = nc.vector.tensor_scalar(nrm[:, b, :], N[:, b * P:(b + 1) * P], mv[:, b, 0:1], rstd[:, b:b + 1],
                                                   ALU.subtract, ALU.mult)
                chain.done(last)
                dve.sem_inc(nrm_done, 1)
                if not gated:
                    dve.sem_inc(rows_free, 1)

            def columns(at, n):
                dve.wait_ge(nt_act, n)
                nc.vector.tensor_tensor(g.xtl[:, at], N, g.xth[:, at].bitcast(F32), ALU.subtract).then_inc(rows_free, 1)

            dve.wait_ge(loaded, LOADS * 16)
            nc.vector.tensor_copy(rw_h[:], rw32[:])
            nc.vector.tensor_copy(ident_r[:], g.ident[:])
            chain.done(nc.vector.tensor_copy(hot[:], hot32[:]))
            if not gated:
                nc.vector.tensor_copy(b2_h[:], b2_32[:])
                chain.done(nc.vector.tensor_tensor(sb2m[:, 0:1], sb2[:, 0:1], sb2[:, 1:2], ALU.add))
                nc.vector.tensor_tensor(b2_l[:], b2_32[:], b2_h[:].bitcast(F32), ALU.subtract)
                nc.vector.tensor_scalar(sb2m[:, 1:2], sb2m[:, 0:1], 1.0 / S1, None, ALU.mult)
            nc.vector.tensor_tensor(rw_l[:], rw32[:], rw_h[:].bitcast(F32), ALU.subtract).then_inc(consts, 1)
            dve.sem_inc(rows_free, 1)
            router_logits(1)
            router_top(1)
            router_weights(1)
            router_columns(1)
            hidden(0, 0)
            hidden(1, 1)
            with dve.Fori(0, NG) as n:
                chain.loop(n, U + 9)
                for u in range(U):
                    if u == 1:
                        router_logits(n + 2)
                    if u == 2:
                        variances(n + 1)
                    if u == 3:
                        router_top(n + 2)
                    if u == 4:
                        normalise(n + 1)
                    if u == 5:
                        router_weights(n + 2)
                    if u == 6 and gated:
                        columns(bass.ds(n * GT, GT), n + 1)
                    if u == 7:
                        router_columns(n + 2)
                    hidden((u + 2) % U, n * U + u + 2)
            chain.end(NG)
            variances(NG + 1)
            normalise(NG + 1)
            if gated:
                columns(slice(NG * GT, (NG + 1) * GT), NG + 1)


def attention1(nc, ctx, g, d):
    sb = lambda name, shape, dt=F32: ctx.enter_context(nc.sbuf_tensor("a1_" + name, shape, dt))
    sem = lambda name: ctx.enter_context(nc.semaphore("a1_" + name))
    SCALE = DH1 ** -0.5
    HG = 4
    NGR = H1 // HG
    NPR = H1 // 2
    VW = 32
    WS = (E1 + S1) * W1C // B
    BT = QB * P

    prob = sb("prob", [P, 2, HG, QB * T])
    sel = sb("sel", [P, 4, NGR, P], F32R)
    pick = sb("pick", [P, H1, P], F32R)
    small32 = sb("small32", [P, 3, P])
    rot = sb("rot", [P, P], F32R)
    ident_r = sb("ident_r", [P, P], F32R)
    wd_h, wd_l = sb("wd_h", [P, 2, P], F32R), sb("wd_l", [P, 2, P], F32R)
    wu = sb("wu", [P, 3, P])
    bias = sb("bias", [P, 4])
    buv = sb("buv", [P, P])
    cos, sin = sb("cos", [P, T]), sb("sin", [P, T])
    lat = sb("lat", [P, 2, T])
    k32, x32 = sb("k32", [P, T]), sb("x32", [P, T])
    xcos, kcos, xsin, ksin = (sb(n, [P, T]) for n in ("xcos", "kcos", "xsin", "ksin"))
    rq, rk = sb("rq", [P, T]), sb("rk", [P, T])
    qk_h, qk_l = sb("qk_h", [P, 2, T], F32R), sb("qk_l", [P, 2, T], F32R)
    qks = sb("qks", [P, 2, NGR, 2 * T], F32R)
    v = sb("v", [P, 2, QB, H1, VW])
    mx = sb("mx", [P, QB, H1])
    mh = sb("mh", [P, QB, 2 * H1], F32R)
    nmx = sb("nmx", [P, QB, H1])
    mt = sb("mt", [P, T], F32R)
    osb = sb("osb", [P, NGR, T])
    rs = sb("rs", [P, QB, H1])
    o = sb("o", [P, QB, P])
    ot = sb("ot", [P, T])
    rt = sb("rt", [P, T])
    stats, mv = sb("stats", [P, QB, 6]), sb("mv", [P, QB, 2])
    veps, rstd, halfs = sb("veps", [P, QB]), sb("rstd", [P, QB]), sb("halfs", [P, QB])
    one = sb("one", [P, 1])
    nrm = sb("nrm", [P, QB, P])
    stage = sb("stage", [P, 2, WS])
    ST = g.psum[:, 0:4, :]
    R0, R1, PV, MISC = (g.psum[:, k, :] for k in (4, 5, 6, 7))

    loaded, consts, dve_chain, pool_chain = sem("loaded"), sem("consts"), sem("dve_chain"), sem("pool_chain")
    lat_ps, lat_done, k_ps, k_done, v_ps, v_done = (sem(n) for n in (
        "lat_ps", "lat_done", "k_ps", "k_done", "v_ps", "v_done"))
    xsin_done, ksin_done, xcos_done, kcos_done, q_split, k_split = (sem(n) for n in (
        "xsin_done", "ksin_done", "xcos_done", "kcos_done", "q_split", "k_split"))
    stack_ps, stack_done, s1_ps, mx_done, nmx_done, mt_ps, mt_done = (sem(n) for n in (
        "stack_ps", "stack_done", "s1_ps", "mx_done", "nmx_done", "mt_ps", "mt_done"))
    st_ps, exp_done, pv_ps, osb_done = (sem(n) for n in ("st_ps", "exp_done", "pv_ps", "osb_done"))
    o_ps, o_done, ot_ps, ot_done, y_ps, rt_done, rows_ps, var_done, rstd_done, nrm_done, ntr_ps, nt_act, nt_done = (
        sem(n) for n in ("o_ps", "o_done", "ot_ps", "ot_done", "y_ps", "rt_done", "rows_ps", "var_done", "rstd_done",
                         "nrm_done", "ntr_ps", "nt_act", "nt_done"))
    stage_in = [sem("stage_in0"), sem("stage_in1")]
    stage_free = sem("stage_free")
    LOADS = 10

    def columns_of(n):
        return bass.ds(n * T + PAD, T)

    with nc.Block() as block:
        @block.sync
        def _(sp):
            flat = prob[:].rearrange("p a h t -> p (a h t)")
            for dst, src in ((flat[:, 0:H1 * P], d["pick"]), (flat[:, H1 * P:2 * H1 * P], d["sel"]), (small32[:], d["small"]),
                             (wu[:, 0, :], d["w_uk"]), (wu[:, 1, :], d["w_uv"]), (wu[:, 2, :], d["w_o"]),
                             (bias[:], d["a1_bias"]), (buv[:], d["b_uv"].partition_broadcast(P)),
                             (cos[:], d["cos"]), (sin[:], d["sin"])):
                sp.dma_start(dst, src).then_inc(loaded, 16)
            with sp.Fori(0, B // 2) as j:
                for half in range(2):
                    n = j * 2 + half
                    sp.wait_ge(stage_free, n + 1)
                    sp.dma_start(stage[:, half, :], d["w1"][:, bass.ds(n * WS, WS)]).then_inc(stage_in[half], 16)

        @block.tensor
        def _(pe):
            def latents(at, n):
                for j in range(2):
                    last = split_mm(nc, MISC[:, j * T:(j + 1) * T], wd_h[:, j, :], wd_l[:, j, :], g.xth[:, at],
                                    g.xtl[:, at], True, True)
                last.then_inc(lat_ps, 1)

            def keys(at, n):
                pe.wait_ge(lat_done, n)
                nc.tensor.matmul(MISC[:, 0:T], wu[:, 0, :], lat[:, 0, :], start=True, stop=True)
                nc.tensor.matmul(MISC[:, T:2 * T], rot[:], g.xth[:, at], start=True, stop=False)
                nc.tensor.matmul(MISC[:, T:2 * T], rot[:], g.xtl[:, at], start=False, stop=True).then_inc(k_ps, 1)

            def values(n):
                pe.wait_ge(k_done, n)
                pe.wait_ge(xsin_done, n)
                for q in range(QB):
                    nc.tensor.matmul(MISC[:, q * P:(q + 1) * P], lat[:, 1, q * P:(q + 1) * P], wu[:, 1, :],
                                     start=True, stop=True)
                nc.tensor.matmul(MISC[:, T:2 * T], small32[:, 2, :], k32[:], start=True, stop=True).then_inc(v_ps, 1)

            def stacks(n):
                pe.wait_ge(q_split, n)
                pe.wait_ge(k_split, n)
                for k in range(NGR):
                    if k >= 2:
                        pe.wait_ge(stack_done, n * NGR + (k - 1 - NGR))
                    for j in range(2):
                        out = (R0, R1)[k % 2][:, j * T:(j + 1) * T]
                        nc.tensor.matmul(out, sel[:, 2 * j, k, :], qk_h[:, j, :], start=True, stop=False)
                        last = nc.tensor.matmul(out, sel[:, 2 * j + 1, k, :], qk_l[:, j, :], start=False, stop=True)
                    last.then_inc(stack_ps, 1)

            def first_scores(h, p, n):
                if h == 0:
                    pe.wait_ge(stack_done, n * NGR)
                if h >= 2:
                    pe.wait_ge(mx_done, n * H1 + (h - 1 - H1))
                rows = slice(32 * (h % HG), 32 * (h % HG) + 32)
                s = qks[rows, p, h // HG, :]
                for q in range(QB):
                    last = nc.tensor.matmul((R0, R1)[h % 2][:, q * T:(q + 1) * T], s[:, q * P:(q + 1) * P], s[:, T:2 * T],
                                            start=True, stop=True, tile_position=(32 * (h % HG), 0))
                last.then_inc(s1_ps, 1)

            def maxima(n):
                pe.wait_ge(nmx_done, n)
                for q in range(QB):
                    last = nc.tensor.transpose(MISC[0:2 * H1, q * P:(q + 1) * P], mh[:, q, :].bitcast(F32), g.ident[:])
                last.then_inc(mt_ps, 1)

            def scores(t, p):
                for h in (2 * t, 2 * t + 1):
                    rows = slice(32 * (h % HG), 32 * (h % HG) + 32)
                    s = qks[rows, p, h // HG, :]
                    for k in range(QB):
                        out = ST[:, 2 * (t % 2) + h % 2, k * T:(k + 1) * T]
                        nc.tensor.matmul(out, s[:, T + k * P:T + (k + 1) * P], s[:, 0:T], start=True, stop=False,
                                         tile_position=(32 * (h % HG), 0))
                        last = nc.tensor.matmul(out, pick[:, h, :], mt[:], start=False, stop=True)
                last.then_inc(st_ps, 1)

            def outputs(k, p, n):
                pe.wait_ge(exp_done, n * NPR + 2 * k + 2)
                pe.wait_ge(osb_done, n * NGR + k + 1)
                for b in range(QB):
                    for j in range(HG):
                        rows = slice(32 * j, 32 * j + 32)
                        last = nc.tensor.matmul(PV[rows, (k % 2) * T:(k % 2 + 1) * T], v[:, p, b, HG * k + j, :],
                                                prob[:, k % 2, j, b * T:(b + 1) * T], start=b == 0, stop=b == QB - 1,
                                                tile_position=(0, 32 * j))
                last.then_inc(pv_ps, 1)

            def tail_heads(n):
                pe.wait_ge(osb_done, n * NGR - (NGR - 1))
                for q in range(QB):
                    for k in range(NGR):
                        last = nc.tensor.transpose((R0, R1)[q][:, k * P:(k + 1) * P], osb[:, k, q * P:(q + 1) * P], g.ident[:])
                last.then_inc(o_ps, 1)

            def tail_columns(n):
                pe.wait_ge(o_done, n)
                for q in range(QB):
                    last = nc.tensor.transpose(R0[:, q * P:(q + 1) * P], o[:, q, :], g.ident[:])
                last.then_inc(ot_ps, 1)

            def tail_project(at, n):
                pe.wait_ge(ot_done, n)
                out = R1[:, 0:T]
                nc.tensor.matmul(out, wu[:, 2, :], ot[:], start=True, stop=False)
                nc.tensor.matmul(out, ident_r[:], g.xth[:, at], start=False, stop=False)
                nc.tensor.matmul(out, ident_r[:], g.xtl[:, at], start=False, stop=True).then_inc(y_ps, 1)

            def tail_rows(n):
                pe.wait_ge(rt_done, n)
                for q in range(QB):
                    last = nc.tensor.transpose(MISC[:, q * P:(q + 1) * P], rt[:, q * P:(q + 1) * P], g.ident[:])
                last.then_inc(rows_ps, 1)

            def tail_store(n):
                pe.wait_ge(nrm_done, n)
                for q in range(QB):
                    last = nc.tensor.transpose(MISC[:, q * P:(q + 1) * P], nrm[:, q, :], g.ident[:])
                last.then_inc(ntr_ps, 1)

            pe.wait_ge(loaded, LOADS * 16)
            pe.wait_ge(consts, 3)
            at = columns_of(0)
            latents(at, 1)
            keys(at, 1)
            values(1)
            stacks(1)
            for h in range(H1):
                first_scores(h, 0, 1)
            maxima(1)
            with pe.Fori(0, B // 2) as i:
                for p in range(2):
                    n = i * 2 + p
                    ahead, behind = columns_of(n + 1), columns_of(n - 1)
                    for t in range(NPR):
                        if t == 0:
                            pe.wait_ge(mt_done, n + 1)
                            pe.wait_ge(v_done, n + 1)
                        if t >= 2:
                            pe.wait_ge(exp_done, n * NPR + t - 1)
                        scores(t, p)
                        if t in (2, 4, 6):
                            outputs(t // 2 - 1, p, n)
                        if t == 0:
                            latents(ahead, n + 2)
                            tail_heads(n + 1)
                        if t == 1:
                            keys(ahead, n + 2)
                            tail_columns(n + 1)
                        if t == 2:
                            values(n + 2)
                            tail_project(behind, n + 1)
                        if t == 3:
                            pe.wait_ge(v_done, n + 2)
                            pe.wait_ge(ksin_done, n + 2)
                            tail_rows(n + 1)
                            stacks(n + 2)
                        if t >= 4:
                            for h in range(4 * (t - 4), 4 * (t - 3)):
                                first_scores(h, 1 - p, n + 2)
                        if t == 5:
                            tail_store(n + 1)
                    outputs(NGR - 1, p, n)
                    pe.wait_ge(nt_done, n + 1)
                    maxima(n + 2)
            tail_heads(B + 1)
            tail_columns(B + 1)
            tail_project(columns_of(B - 1), B + 1)
            tail_rows(B + 1)
            tail_store(B + 1)

        @block.scalar
        def _(act):
            def latents(n):
                act.wait_ge(lat_ps, n)
                for j in range(2):
                    last = nc.scalar.activation(lat[:, j, :], MISC[:, j * T:(j + 1) * T], ACT.Identity, bias=bias[:, j:j + 1])
                last.then_inc(lat_done, 1)

            def keys(n):
                act.wait_ge(k_ps, n)
                nc.scalar.activation(k32[:], MISC[:, 0:T], ACT.Identity, bias=bias[:, 2:3]).then_inc(k_done, 1)

            def stacks(p, n):
                for k in range(NGR):
                    act.wait_ge(stack_ps, n * NGR + (k + 1 - NGR))
                    nc.scalar.activation(qks[:, p, k, :], (R0, R1)[k % 2], ACT.Copy).then_inc(stack_done, 1)

            def exps(t, n):
                act.wait_ge(st_ps, n * NPR + t + 1)
                k = t // 2
                nc.scalar.activation(prob[:, k % 2, 2 * (t % 2):2 * (t % 2) + 2, :], ST[:, 2 * (t % 2):2 * (t % 2) + 2, :],
                                     ACT.Exp, scale=SCALE).then_inc(exp_done, 1)

            def outputs(k, n):
                act.wait_ge(pv_ps, n * NGR + k + 1)
                nc.scalar.activation(osb[:, k, :], PV[:, (k % 2) * T:(k % 2 + 1) * T], ACT.Copy).then_inc(osb_done, 1)

            def tail_columns(n):
                act.wait_ge(ot_ps, n)
                nc.scalar.activation(ot[:], R0[:, 0:T], ACT.Copy).then_inc(ot_done, 1)

            def tail_residual(n):
                act.wait_ge(y_ps, n)
                nc.scalar.activation(rt[:], R1[:, 0:T], ACT.Identity, bias=bias[:, 3:4]).then_inc(rt_done, 1)

            def tail_store(at, n):
                act.wait_ge(ntr_ps, n)
                nc.scalar.activation(g.xth[:, at], MISC[:, 0:T], ACT.Copy).then_inc(nt_act, 1)

            act.wait_ge(loaded, LOADS * 16)
            act.wait_ge(consts, 3)
            latents(1)
            keys(1)
            stacks(0, 1)
            with act.Fori(0, B // 2) as i:
                for p in range(2):
                    n = i * 2 + p
                    for t in range(NPR):
                        exps(t, n)
                        if t in (2, 4, 6):
                            outputs(t // 2 - 1, n)
                        if t == 0:
                            latents(n + 2)
                        if t == 1:
                            keys(n + 2)
                            tail_columns(n + 1)
                        if t == 2:
                            tail_residual(n + 1)
                        if t == 3:
                            stacks(1 - p, n + 2)
                        if t == 6:
                            tail_store(columns_of(n - 1), n + 1)
                    outputs(NGR - 1, n)
            tail_columns(B + 1)
            tail_residual(B + 1)
            tail_store(columns_of(B - 1), B + 1)

        @block.gpsimd
        def _(pool):
            def rotate_x(at, n, count):
                if not isinstance(n, int):
                    pool.wait_ge(q_split, n - 1)
                nc.gpsimd.tensor_tensor(x32[:], g.xth[:, at].bitcast(F32), g.xtl[:, at].bitcast(F32), ALU.add
                                        ).then_inc(pool_chain, 1)
                pool.wait_ge(pool_chain, count)
                nc.gpsimd.tensor_tensor(xcos[:], x32[:], cos[:], ALU.mult).then_inc(xcos_done, 1)

            def rotate_k(n):
                pool.wait_ge(k_done, n)
                if not isinstance(n, int):
                    pool.wait_ge(k_split, n - 1)
                nc.gpsimd.tensor_tensor(kcos[:], k32[:], cos[:], ALU.mult).then_inc(kcos_done, 1)

            def power(n):
                pool.wait_ge(var_done, n)
                nc.gpsimd.tensor_tensor(rstd[:], veps[:], halfs[:], ALU.pow).then_inc(rstd_done, 1)

            nc.gpsimd.memset(one[:], 1.0)
            nc.gpsimd.memset(halfs[:], -0.5).then_inc(consts, 1)
            pool.sem_inc(stage_free, 2)
            pool.wait_ge(loaded, LOADS * 16)
            rotate_x(columns_of(0), 1, 1)
            rotate_k(1)
            with pool.Fori(0, B // 2) as i:
                for half in range(2):
                    n = i * 2 + half
                    rotate_x(columns_of(n + 1), n + 2, n * 2 + 2)
                    rotate_k(n + 2)
                    power(n + 1)
                    at = bass.ds(n * WS, WS)
                    pool.wait_ge(stage_in[half], (i + 1) * 16)
                    nc.gpsimd.tensor_tensor(g.wh[:, at], stage[:, half, :], one[:].to_broadcast(stage[:, half, :].shape), ALU.mult).then_inc(pool_chain, 1)
                    pool.wait_ge(pool_chain, n * 2 + 3)
                    nc.gpsimd.tensor_tensor(g.wl[:, at], stage[:, half, :], g.wh[:, at].bitcast(F32),
                                            ALU.subtract).then_inc(stage_free, 1)
            power(B + 1)

        @block.vector
        def _(dve):
            chain = Counter(dve, dve_chain)

            def rotate(j, turned, sine, cosine, total, signal, n):
                chain.done(nc.vector.tensor_tensor(sine[:], turned, sin[:], ALU.mult))
                dve.sem_inc(signal[0], 1)
                dve.wait_ge(signal[1], n)
                chain.done(nc.vector.tensor_tensor(total[:], sine[:], cosine[:], ALU.add))
                chain.done(nc.vector.tensor_copy(qk_h[:, j, :], total[:]))
                nc.vector.tensor_tensor(qk_l[:, j, :], total[:], qk_h[:, j, :].bitcast(F32), ALU.subtract
                                        ).then_inc(signal[2], 1)

            def rotate_q(n):
                dve.wait_ge(k_done, n)
                rotate(0, MISC[:, T:2 * T], xsin, xcos, rq, (xsin_done, xcos_done, q_split), n)

            def values(p, n):
                dve.wait_ge(v_ps, n)
                nc.vector.tensor_tensor(v[:, p, :, :, 0:DH1], MISC[:, 0:BT].rearrange("p (q h e) -> p q h e", q=QB, h=H1),
                                        buv[:].rearrange("p (a h e) -> p a h e", a=1, h=H1).to_broadcast([P, QB, H1, DH1]),
                                        ALU.add).then_inc(v_done, 1)
                rotate(1, MISC[:, T:2 * T], ksin, kcos, rk, (ksin_done, kcos_done, k_split), n)

            def maxima(h, n):
                dve.wait_ge(s1_ps, n * H1 + (h + 1 - H1))
                nc.vector.reduce_max(mx[:, :, h:h + 1], (R0, R1)[h % 2].rearrange("p (q k) -> p q k", q=QB), AX.X
                                     ).then_inc(mx_done, 1)

            def negate(n):
                dve.wait_ge(mx_done, n * H1)
                nc.vector.tensor_scalar(mh[:, :, 0:H1], mx[:], -1.0, None, ALU.mult)
                chain.done(nc.vector.tensor_scalar(nmx[:], mx[:], -1.0, None, ALU.mult))
                nc.vector.tensor_tensor(mh[:, :, H1:2 * H1], nmx[:], mh[:, :, 0:H1].bitcast(F32), ALU.subtract
                                        ).then_inc(nmx_done, 1)
                dve.wait_ge(mt_ps, n)
                nc.vector.tensor_copy(mt[0:2 * H1, :], MISC[0:2 * H1, 0:T]).then_inc(mt_done, 1)

            def tail_heads(n):
                dve.wait_ge(o_ps, n)
                by_head = [r.rearrange("p (h e) -> p h e", h=H1) for r in (R0, R1)]
                for q in range(QB):
                    last = nc.vector.reciprocal(rs[:, q, :], by_head[q][:, :, DH1])
                chain.done(last)
                for q in range(QB):
                    last = nc.vector.tensor_tensor(o[:, q, :].rearrange("p (h e) -> p h e", h=H1), by_head[q][:, :, 0:DH1],
                                                   rs[:, q, :].rearrange("p (h a) -> p h a", a=1).to_broadcast([P, H1, DH1]),
                                                   ALU.mult)
                last.then_inc(o_done, 1)

            def variances(n):
                dve.wait_ge(rows_ps, n)
                for q in range(QB):
                    last = nc.vector.bn_stats(stats[:, q, :], MISC[:, q * P:(q + 1) * P])
                chain.done_apart(last, g.spare[:])
                for q in range(QB):
                    last = nc.vector.bn_aggr(mv[:, q, :], stats[:, q:q + 1, :])
                chain.done(last)
                nc.vector.tensor_scalar(veps[:], mv[:, :, 1], EPS, None, ALU.add).then_inc(var_done, 1)

            def normalise(n):
                dve.wait_ge(rstd_done, n)
                for q in range(QB):
                    last = nc.vector.tensor_scalar(nrm[:, q, :], MISC[:, q * P:(q + 1) * P], mv[:, q, 0:1], rstd[:, q:q + 1],
                                                   ALU.subtract, ALU.mult)
                last.then_inc(nrm_done, 1)

            def tail_store(at, n):
                dve.wait_ge(nt_act, n)
                nc.vector.tensor_tensor(g.xtl[:, at], MISC[:, 0:T], g.xth[:, at].bitcast(F32), ALU.subtract
                                        ).then_inc(nt_done, 1)

            chain.done(nc.vector.memset(v[:], 0.0))
            nc.vector.memset(v[:, :, :, :, DH1:DH1 + 1], 1.0)
            nc.vector.memset(osb[:], 1.0)
            nc.vector.memset(mt[:].bitcast(F32), 0.0).then_inc(osb_done, 1)
            dve.wait_ge(loaded, LOADS * 16)
            flat = prob[:].rearrange("p a h t -> p (a h t)")
            nc.vector.tensor_copy(pick[:].rearrange("p h n -> p (h n)"), flat[:, 0:H1 * P])
            nc.vector.tensor_copy(sel[:].rearrange("p a k n -> p (a k n)"), flat[:, H1 * P:2 * H1 * P]).then_inc(consts, 1)
            nc.vector.tensor_copy(wd_h[:], small32[:, 0:2, :])
            nc.vector.tensor_copy(ident_r[:], g.ident[:])
            chain.done(nc.vector.tensor_copy(rot[:], small32[:, 2, :]))
            nc.vector.tensor_tensor(wd_l[:], small32[:, 0:2, :], wd_h[:].bitcast(F32), ALU.subtract).then_inc(consts, 1)
            rotate_q(1)
            values(0, 1)
            for h in range(H1):
                maxima(h, 1)
            negate(1)
            with dve.Fori(0, B // 2) as i:
                chain.loop(i, 2 * 10)
                for p in range(2):
                    n = i * 2 + p
                    tail_heads(n + 1)
                    rotate_q(n + 2)
                    values(1 - p, n + 2)
                    variances(n + 1)
                    for t in range(4, NPR):
                        for h in range(4 * (t - 4), 4 * (t - 3)):
                            maxima(h, n + 2)
                        if t == 4:
                            normalise(n + 1)
                        if t == 6:
                            tail_store(columns_of(n - 1), n + 1)
                    negate(n + 2)
            chain.end(B // 2)
            tail_heads(B + 1)
            variances(B + 1)
            normalise(B + 1)
            tail_store(columns_of(B - 1), B + 1)


PHASES = 4
INS = dict(x="L0_attn_x", wq="L0_attn_Wq", wk="L0_attn_Wk", wv="L0_attn_Wv", wo="L0_attn_Wo")


def layout(inputs):
    import numpy as np

    a = {k: np.ascontiguousarray(inputs[name]) for k, name in INS.items()}
    columns = lambda *names: np.ascontiguousarray(np.stack([np.reshape(inputs[n], (-1, P)).T for n in names], axis=1))
    a["bqkv"] = columns("L0_attn_bq", "L0_attn_bk", "L0_attn_bv")
    gate, up = (np.transpose(inputs[n], (2, 0, 1)) for n in ("L0_ffn_gate_w", "L0_ffn_up_w"))
    down = np.transpose(np.reshape(inputs["L0_ffn_down_w"], (E0, P, FB0, P)), (3, 0, 2, 1)).reshape(P, E0, FB0 * P)
    a["w0"] = np.ascontiguousarray(np.concatenate([gate, up, down], axis=2).reshape(P, E0 * W0C))
    a["ident"] = np.eye(P, dtype=np.float32)
    r = np.arange(P)
    a["iota"] = np.tile(np.arange(E0, dtype=np.float32), (P, 1))
    hot = np.zeros((E0, E0, P), np.float32)
    hot[np.arange(E0), np.arange(E0)] = 1
    a["hot"] = hot
    a["zeros"] = np.zeros((P, GT), np.float32)
    for tag, router in (("m0_", np.transpose(inputs["L0_ffn_router_w"])), ("m1_", inputs["L1_ffn_router_w"])):
        a[tag + "rw"] = np.zeros((P, P), np.float32)
        a[tag + "rw"][:, :E0] = router
        a[tag + "rb"] = np.zeros((P, 1), np.float32)
        a[tag + "rb"][:E0, 0] = inputs[f"L{tag[1]}_ffn_router_b"]
    turn = np.zeros((P, P), np.float32)
    half = DH1 // 2
    for m in range(P):
        turn[m + half if m % DH1 < half else m - half, m] = -1 if m % DH1 < half else 1
    a["small"] = np.ascontiguousarray(np.stack([inputs["L1_attn_w_dk"], inputs["L1_attn_w_dv"], turn], axis=1))
    for n in ("w_uk", "w_uv", "w_o", "b_uv"):
        a[n] = np.ascontiguousarray(inputs["L1_attn_" + n])
    a["a1_bias"] = np.ascontiguousarray(np.stack([inputs["L1_attn_" + n] for n in ("b_dk", "b_dv", "b_uk", "b_o")], axis=1))
    inv = np.float32(1) / np.float32(10000) ** (np.arange(0, DH1, 2, dtype=np.float32) / np.float32(DH1))
    angle = np.tile(inv.astype(np.float32), P // half)[:, None] * np.arange(T, dtype=np.float32)[None, :]
    a["cos"], a["sin"] = np.cos(angle), np.sin(angle)
    sel = np.zeros((P, 4, H1 // 4, P), np.float32)
    for f in range(P):
        h, e = f // DH1, f % DH1
        for c in range(4):
            for j, high in ((0, c in (0, 2)), (1, c in (0, 1))):
                sel[f, 2 * j + (0 if high else 1), h // 4, 32 * (h % 4) + 8 * c + e] = 1
    a["sel"] = sel.reshape(P, -1)
    pick = np.zeros((P, H1, P), np.float32)
    for h in range(H1):
        pick[h, h] = pick[H1 + h, h] = 1
    a["pick"] = pick.reshape(P, -1)
    up = np.transpose(np.concatenate([inputs["L1_ffn_w1"], inputs["L1_ffn_sw1"]]), (1, 0, 2))
    down = np.transpose(np.concatenate([inputs["L1_ffn_w2"], inputs["L1_ffn_sw2"]]).reshape(E1 + S1, FB1, P, P),
                        (2, 0, 1, 3)).reshape(P, E1 + S1, FB1 * P)
    a["w1"] = np.ascontiguousarray(np.concatenate([up, down], axis=2).reshape(P, (E1 + S1) * W1C))
    b1 = np.concatenate([inputs["L1_ffn_b1"], inputs["L1_ffn_sb1"]])
    a["m1_b1"] = np.ascontiguousarray(b1.reshape(-1, P).T)
    a["m1_b2"] = np.ascontiguousarray(inputs["L1_ffn_b2"])
    a["m1_sb2"] = np.ascontiguousarray(inputs["L1_ffn_sb2"].T)
    a["mask"] = np.where(r[None, :] > r[:, None], np.float32(MASKED), np.float32(0))
    return a


def program(nc, d, phases=PHASES):
    with ExitStack() as ctx:
        g = Shared()

        def weights(c, tag, width):
            g.wh = c.enter_context(nc.sbuf_tensor("wh" + tag, [P, width], F32R))
            g.wl = c.enter_context(nc.sbuf_tensor("wl" + tag, [P, width], F32R))

        g.psum = ctx.enter_context(nc.psum_tensor("psum", [P, 8, 512], F32))
        g.spare = ctx.enter_context(nc.sbuf_tensor("spare", [P, 1], F32))
        g.ident = ctx.enter_context(nc.sbuf_tensor("ident", [P, P], F32))
        g.xth = ctx.enter_context(nc.sbuf_tensor("xth", [P, XC], F32R))
        g.xtl = ctx.enter_context(nc.sbuf_tensor("xtl", [P, XC], F32R))
        with ExitStack() as c:
            weights(c, "0", E0 * W0C)
            with ExitStack() as a:
                attention0(nc, a, g, d)
            if phases >= 2:
                moe(nc, c, g, d, "m0_", True)
        if phases >= 3:
            with ExitStack() as c:
                weights(c, "1", (E1 + S1) * W1C)
                with ExitStack() as a:
                    attention1(nc, a, g, d)
                if phases >= 4:
                    moe(nc, c, g, d, "m1_", False)
        if phases < PHASES:
            with nc.semaphore("dbg") as s, nc.Block() as block:
                @block.sync
                def _(sp):
                    sp.dma_start(d["dbg"][0][:, PAD:], g.xth[:, PAD:].bitcast(F32)).then_inc(s, 16)
                    sp.dma_start(d["dbg"][1][:, PAD:], g.xtl[:, PAD:].bitcast(F32)).then_inc(s, 16)
                    sp.wait_ge(s, 32)


def kernel(**inputs):
    import numpy as np
    from concourse import bacc
    from concourse.bass_utils import run_bass_kernel_spmd

    nc = bacc.Bacc("TRN2", target_bir_lowering=False, num_devices=1)
    arrays = layout({name: np.asarray(a) for name, a in inputs.items()})
    d = {k: nc.dram_tensor("in_" + k, a.shape, mybir.dt.from_np(a.dtype), kind="ExternalInput").ap()
         for k, a in arrays.items()}
    d["out"] = nc.dram_tensor("out", (GT + NT, P), F32, kind="ExternalOutput").ap()
    program(nc, d)
    r = run_bass_kernel_spmd(nc, [{"in_" + k: a for k, a in arrays.items()}], core_ids=[0])
    return r.results[0]["out"][GT:].reshape(B, T, P)
```

```python
from contextlib import ExitStack

import concourse.bass as bass
from concourse import mybir

F32 = mybir.dt.float32
F32R = mybir.dt.float32r
BF16 = mybir.dt.bfloat16
U32 = mybir.dt.uint32
ALU = mybir.AluOpType
ACT = mybir.ActivationFunctionType
AX = mybir.AxisListType

P = 128
B, T = 16, 256
NT = B * T
QB = T // P
GT = 512
NG = NT // GT
GB = GT // P
EPS = 1e-5
PAD = GT
XC = PAD + NT + PAD

H0, DK0 = 16, 64
HP = H0 // 2
E0, F0 = 8, 512
FB0 = F0 // P
W0C = 2 * F0 + FB0 * P
H1, DH1 = 16, 8
E1, F1, S1 = 8, 256, 2
FB1 = F1 // P
W1C = F1 + FB1 * P
LOW = 32
HOT_ROWS = LOW + E0
MASKED = -(2.0 ** 120)


class Counter:

    def __init__(self, eng, sem):
        self.eng, self.sem, self.base, self.per, self.k, self.i = eng, sem, 0, 0, 0, None

    def loop(self, i, per):
        assert self.i is None
        self.base, self.k, self.i, self.per = self.base + self.k, 0, i, per

    def end(self, count):
        assert self.k == self.per, (self.k, self.per)
        self.base, self.k, self.i = self.base + self.per * count, 0, None

    def value(self):
        v = self.base + self.k
        return v if self.i is None else self.i * self.per + v

    def done(self, ins):
        self.k += 1
        ins.then_inc(self.sem, 1)
        self.eng.wait_ge(self.sem, self.value())

    def done_apart(self, ins, spare):
        self.done(ins)
        self.eng.memset(spare, 0.0)


def split_mm(nc, out, wh, wl, xh, xl, start, stop):
    nc.tensor.matmul(out, wh, xh, start=start, stop=False)
    nc.tensor.matmul(out, wl, xh, start=False, stop=False)
    return nc.tensor.matmul(out, wh, xl, start=False, stop=stop)


class Shared:
    pass


def attention0(nc, ctx, g, d):
    sb = lambda name, shape, dt=F32: ctx.enter_context(nc.sbuf_tensor("a0_" + name, shape, dt))
    sem = lambda name: ctx.enter_context(nc.semaphore("a0_" + name))
    SCALE = DK0 ** -0.5
    SW = 3 * P

    wqk_h = sb("wqk_h", [P, 2, H0 * DK0], F32R)
    wqk_l = sb("wqk_l", [P, 2, H0 * DK0], F32R)
    wv = sb("wv", [P, H0 * DK0])
    wo = sb("wo", [P, HP, P])
    bias = sb("bias", [P, 3, HP])
    mask32 = sb("mask32", [P, P])
    mask = sb("mask", [P, P], BF16)
    identb = sb("identb", [P, P], BF16)
    xin = sb("xin", [P, QB, P])
    xres = sb("xres", [P, QB, P])
    xt = sb("xt", [P, T])
    xt_h = sb("xt_h", [P, T], F32R)
    xt_l = sb("xt_l", [P, T], F32R)
    qkt = sb("qkt", [P, 2, 2, T])
    v = sb("v", [P, 4, QB, P])
    prob = sb("prob", [P, 2, 2, SW])
    probt = sb("probt", [P, 2, 2, SW])
    mx = sb("mx", [P, 2, 2, 2])
    nmx = sb("nmx", [P, 2, 2, 2])
    lsum = sb("lsum", [P, 2, 2, 2])
    rl = sb("rl", [P, 2, 2, 2])
    ot = sb("ot", [P, HP, T])
    w32 = ot[:].rearrange("p (a h) t -> p a (h t)", a=2)
    res = sb("res", [P, QB, P])
    stats = sb("stats", [P, QB, 6])
    mv = sb("mv", [P, QB, 2])
    veps = sb("veps", [P, QB])
    rstd = sb("rstd", [P, QB])
    halfs = sb("halfs", [P, QB])
    one = sb("one", [P, 1])
    nrm = sb("nrm", [P, QB, P])
    stage = sb("stage", [P, 2, W0C // 2])
    S = g.psum[:, 0:4, :]
    PT = g.psum[:, 4:6, :]
    QK = g.psum[:, 6, :]
    VO = g.psum[:, 7, :]

    loaded_c, loaded_w, x_in = sem("loaded_c"), sem("loaded_w"), sem("x_in")
    consts, w_split = sem("consts"), sem("w_split")
    xtr_ps, xt_act, xt_done = sem("xtr_ps"), sem("xt_act"), sem("xt_done")
    qk_ps, qk_done, v_ps, v_done = sem("qk_ps"), sem("qk_done"), sem("v_ps"), sem("v_done")
    sc_ps, nmx_done, exp_done, prob_done = sem("sc_ps"), sem("nmx_done"), sem("exp_done"), sem("prob_done")
    pt_ps, pt_done, pv_ps, ot_done = sem("pt_ps"), sem("pt_done"), sem("pv_ps"), sem("ot_done")
    y_ps, res_done, xres_done = sem("y_ps"), sem("res_done"), sem("xres_done")
    var_done, rstd_done, nrm_done = sem("var_done"), sem("rstd_done"), sem("nrm_done")
    ntr_ps, nt_act, nt_done = sem("ntr_ps"), sem("nt_act"), sem("nt_done")
    init, dve_chain, pool_chain = sem("init"), sem("dve_chain"), sem("pool_chain")
    stage_in = [sem("stage_in0"), sem("stage_in1")]
    stage_free = sem("stage_free")
    x_d = d["x"].rearrange("b (q p) f -> b p q f", p=P)

    with nc.Block() as block:
        @block.sync
        def _(sp):
            sp.dma_start(xin[:], x_d[0]).then_inc(x_in, 16)
            sp.dma_start(w32[:, 0, :], d["wq"]).then_inc(loaded_w, 16)
            sp.dma_start(w32[:, 1, :], d["wk"]).then_inc(loaded_w, 16)
            sp.dma_start(bias[:], d["bqkv"]).then_inc(loaded_c, 16)
            sp.dma_start(wo[:], d["wo"].rearrange("(h p) n -> p h n", p=P)).then_inc(loaded_c, 16)

            def loads(j, last=False):
                for half in range(2):
                    i = j * 2 + half
                    sp.wait_ge(stage_free, i + 1)
                    sp.dma_start(stage[:, half, :], d["w0"][:, bass.ds(i * (W0C // 2), W0C // 2)]
                                 ).then_inc(stage_in[half], 16)
                    sp.wait_ge(xres_done, i + 2)
                    sp.wait_ge(xtr_ps, i + 1)
                    nxt = 0 if last and half else i + 1
                    sp.dma_start(xin[:], x_d[bass.ds(nxt, 1)].rearrange("a p q f -> p (a q) f")).then_inc(x_in, 16)

            with sp.Fori(0, B // 2 - 1) as j:
                loads(j)
            loads(B // 2 - 1, last=True)

        @block.scalar
        def _(act):
            act.dma_start(g.ident[:], d["ident"]).then_inc(loaded_c, 16)
            act.dma_start(mask32[:], d["mask"]).then_inc(loaded_c, 16)
            act.dma_start(wv[:], d["wv"]).then_inc(loaded_c, 16)
            act.wait_ge(loaded_w, 32)
            nc.scalar.activation(wqk_h[:], w32, ACT.Copy).then_inc(w_split, 1)

            def activations():
                nc.scalar.activation(xt[:], QK[:, 0:T], ACT.Copy).then_inc(xt_act, 1)
                nc.scalar.activation(xt_h[:], QK[:, 0:T], ACT.Copy).then_inc(xt_act, 1)

            def exps(slot, h):
                for q in range(QB):
                    at = slice(0, P) if q == 0 else slice(P, SW)
                    last = nc.scalar.activation(prob[:, slot, h, at], S[:, 2 * slot + h, at], ACT.Exp,
                                                bias=nmx[:, slot, q, h:h + 1], scale=SCALE,
                                                accum_out=lsum[:, slot, h, q:q + 1])
                last.then_inc(exp_done, 1)

            act.wait_ge(xtr_ps, 1)
            activations()
            act.wait_ge(nmx_done, 1)
            exps(0, 0)
            exps(0, 1)
            act.sem_inc(ot_done, 1)
            with act.Fori(0, B) as i:
                for hp in range(HP):
                    s = i * HP + hp
                    act.wait_ge(nmx_done, s + 2)
                    exps((hp + 1) % 2, 0)
                    act.wait_ge(pt_ps, s + 1)
                    nc.scalar.activation(probt[:, hp % 2], PT[:, :, 0:SW], ACT.Copy).then_inc(pt_done, 1)
                    if hp == 2:
                        act.wait_ge(ntr_ps, i + 1)
                        nc.scalar.activation(g.xth[:, bass.ds(i * T + (PAD - T), T)], QK[:, 0:T],
                                             ACT.Copy).then_inc(nt_act, 1)
                    if hp == 5:
                        act.wait_ge(xtr_ps, i + 2)
                        activations()
                    exps((hp + 1) % 2, 1)
                    if hp == 0:
                        act.wait_ge(y_ps, i + 1)
                    act.wait_ge(pv_ps, s + 1)
                    nc.scalar.activation(ot[:, hp, :], VO[:, 0:T], ACT.Identity,
                                         bias=bias[:, 2, hp:hp + 1]).then_inc(ot_done, 1)
            act.wait_ge(ntr_ps, B + 1)
            nc.scalar.activation(g.xth[:, PAD + NT - T:PAD + NT], QK[:, 0:T], ACT.Copy).then_inc(nt_act, 1)

        @block.gpsimd
        def _(pool):
            nc.gpsimd.memset(halfs[:], -0.5)
            nc.gpsimd.memset(one[:], 1.0)
            nc.gpsimd.memset(g.xth[:, PAD + NT:XC].bitcast(F32), 0.0)
            nc.gpsimd.memset(g.xtl[:, PAD + NT:XC].bitcast(F32), 0.0)
            pool.wait_ge(x_in, 16)
            nc.gpsimd.tensor_copy(xres[:], xin[:]).then_inc(xres_done, 1)
            pool.sem_inc(stage_free, 2)
            with pool.Fori(0, B // 2) as j:
                for half in range(2):
                    i = j * 2 + half
                    pool.wait_ge(x_in, i * 16 + 16)
                    pool.wait_ge(res_done, i + 1)
                    nc.gpsimd.tensor_tensor(xres[:], xin[:], one[:].unsqueeze(2).to_broadcast([P, QB, P]), ALU.mult
                                            ).then_inc(xres_done, 1)
                    pool.wait_ge(var_done, i + 1)
                    nc.gpsimd.tensor_tensor(rstd[:], veps[:], halfs[:], ALU.pow).then_inc(rstd_done, 1)
                    at = bass.ds(i * (W0C // 2), W0C // 2)
                    pool.wait_ge(stage_in[half], (j + 1) * 16)
                    nc.gpsimd.tensor_tensor(g.wh[:, at], stage[:, half, :], one[:].to_broadcast(stage[:, half, :].shape), ALU.mult).then_inc(pool_chain, 1)
                    pool.wait_ge(pool_chain, i + 1)
                    nc.gpsimd.tensor_tensor(g.wl[:, at], stage[:, half, :], g.wh[:, at].bitcast(F32),
                                            ALU.subtract).then_inc(stage_free, 1)
            pool.wait_ge(var_done, B + 1)
            nc.gpsimd.tensor_tensor(rstd[:], veps[:], halfs[:], ALU.pow).then_inc(rstd_done, 1)

        @block.vector
        def _(dve):
            chain = Counter(dve, dve_chain)
            dve.wait_ge(loaded_c, 5 * 16)
            nc.vector.tensor_copy(mask[:], mask32[:]).then_inc(consts, 1)
            nc.vector.tensor_copy(identb[:], g.ident[:]).then_inc(consts, 1)
            dve.wait_ge(w_split, 1)
            nc.vector.tensor_tensor(wqk_l[:], w32, wqk_h[:].bitcast(F32), ALU.subtract).then_inc(w_split, 1)

            def activations(n):
                dve.wait_ge(xt_act, n)
                nc.vector.tensor_tensor(xt_l[:], xt[:], xt_h[:].bitcast(F32), ALU.subtract).then_inc(xt_done, 1)

            def evac_qk(hp, n):
                dve.wait_ge(qk_ps, n)
                for j in range(2):
                    last = nc.vector.tensor_scalar(qkt[:, hp % 2, j, :], QK[:, j * T:(j + 1) * T],
                                                   bias[:, j, hp % HP:hp % HP + 1], None, ALU.add)
                last.then_inc(qk_done, 1)

            def evac_v(hp, n):
                dve.wait_ge(v_ps, n)
                nc.vector.tensor_copy(v[:, hp % 4], VO[:, 0:QB * P].rearrange("p (q n) -> p q n", q=QB)
                                      ).then_inc(v_done, 1)

            def maxima(slot, n):
                dve.wait_ge(sc_ps, n)
                nc.vector.reduce_max(mx[:, slot, 0, :], S[:, 2 * slot:2 * slot + 2, 0:P], AX.X)
                chain.done(nc.vector.reduce_max(mx[:, slot, 1, :], S[:, 2 * slot:2 * slot + 2, P:SW], AX.X))
                nc.vector.tensor_scalar(nmx[:, slot], mx[:, slot], -SCALE, None, ALU.mult).then_inc(nmx_done, 1)

            def normalise(slot, h, n):
                dve.wait_ge(exp_done, n)
                chain.done(nc.vector.reciprocal(rl[:, slot, h, :], lsum[:, slot, h, :]))
                nc.vector.tensor_scalar(prob[:, slot, h, 0:P], prob[:, slot, h, 0:P], rl[:, slot, h, 0:1], None, ALU.mult)
                nc.vector.tensor_scalar(prob[:, slot, h, P:SW], prob[:, slot, h, P:SW], rl[:, slot, h, 1:2], None,
                                        ALU.mult).then_inc(prob_done, 1)

            def residual(n):
                dve.wait_ge(y_ps, n)
                dve.wait_ge(xres_done, n)
                chain.done(nc.vector.tensor_tensor(res[:], QK[:, 0:QB * P].rearrange("p (q n) -> p q n", q=QB), xres[:],
                                                   ALU.add))
                dve.sem_inc(res_done, 1)
                for q in range(QB):
                    last = nc.vector.bn_stats(stats[:, q, :], res[:, q, :])
                chain.done_apart(last, g.spare[:])
                for q in range(QB):
                    last = nc.vector.bn_aggr(mv[:, q, :], stats[:, q:q + 1, :])
                chain.done(last)
                nc.vector.tensor_scalar(veps[:], mv[:, :, 1], EPS, None, ALU.add).then_inc(var_done, 1)

            def layernorm():
                for q in range(QB):
                    last = nc.vector.tensor_scalar(nrm[:, q, :], res[:, q, :], mv[:, q, 0:1], rstd[:, q:q + 1],
                                                   ALU.subtract, ALU.mult)
                last.then_inc(nrm_done, 1)

            activations(2)
            evac_qk(0, 1)
            evac_v(0, 1)
            evac_qk(1, 2)
            evac_v(1, 2)
            maxima(0, 1)
            evac_qk(2, 3)
            evac_v(2, 3)
            maxima(1, 2)
            normalise(0, 0, 1)
            normalise(0, 1, 2)
            with dve.Fori(0, B) as i:
                chain.loop(i, HP * 3 + 3)
                for hp in range(HP):
                    s = i * HP + hp
                    normalise((hp + 1) % 2, 0, s * 2 + 3)
                    maxima(hp % 2, s + 3)
                    if hp == 2:
                        dve.wait_ge(nt_act, i + 1)
                        at = bass.ds(i * T + (PAD - T), T)
                        nc.vector.tensor_tensor(g.xtl[:, at], QK[:, 0:T], g.xth[:, at].bitcast(F32),
                                                ALU.subtract).then_inc(nt_done, 1)
                    if hp == 5:
                        activations(i * 2 + 4)
                    normalise((hp + 1) % 2, 1, s * 2 + 4)
                    if hp == 0:
                        residual(i + 1)
                    if hp == 1:
                        dve.wait_ge(rstd_done, i + 1)
                        layernorm()
                    evac_qk(hp + 3, s + 4)
                    evac_v(hp + 3, s + 4)
            chain.end(B)
            residual(B + 1)
            dve.wait_ge(rstd_done, B + 1)
            layernorm()
            dve.wait_ge(nt_act, B + 1)
            nc.vector.tensor_tensor(g.xtl[:, PAD + NT - T:PAD + NT], QK[:, 0:T], g.xth[:, PAD + NT - T:PAD + NT].bitcast(F32),
                                    ALU.subtract).then_inc(nt_done, 1)

        @block.tensor
        def _(pe):
            def rows_to_columns(src, signal):
                for q in range(QB):
                    last = nc.tensor.transpose(QK[:, q * P:(q + 1) * P], src[:, q, :], g.ident[:])
                last.then_inc(signal, 1)

            def project_qk(hp):
                hp = hp % HP
                at = slice(hp * P, (hp + 1) * P)
                for j in range(2):
                    last = split_mm(nc, QK[:, j * T:(j + 1) * T], wqk_h[:, j, at], wqk_l[:, j, at], xt_h[:], xt_l[:],
                                    True, True)
                last.then_inc(qk_ps, 1)

            def project_v(hp):
                hp = hp % HP
                for q in range(QB):
                    last = nc.tensor.matmul(VO[:, q * P:(q + 1) * P], xt[:, q * P:(q + 1) * P], wv[:, hp * P:(hp + 1) * P],
                                            start=True, stop=True)
                last.then_inc(v_ps, 1)

            def scores(slot, hp):
                for h in range(2):
                    row = slice(h * DK0, (h + 1) * DK0)
                    out = S[:, 2 * slot + h, :]
                    q, k = qkt[row, hp % 2, 0, :], qkt[row, hp % 2, 1, :]
                    nc.tensor.matmul(out[:, 0:P], q[:, 0:P], k[:, 0:P], start=True, stop=True)
                    nc.tensor.matmul(out[:, P:SW], q[:, P:T], k, start=True, stop=False)
                    last = nc.tensor.matmul(out[:, 2 * P:SW], identb[:], mask[:], start=False, stop=True)
                last.then_inc(sc_ps, 1)

            def output(n, signal):
                pe.wait_ge(ot_done, n)
                for q in range(QB):
                    for hp in range(HP):
                        last = nc.tensor.matmul(QK[:, q * P:(q + 1) * P], ot[:, hp, q * P:(q + 1) * P], wo[:, hp, :],
                                                start=hp == 0, stop=hp == HP - 1)
                last.then_inc(signal, 1)

            pe.wait_ge(loaded_c, 5 * 16)
            pe.wait_ge(x_in, 16)
            rows_to_columns(xin, xtr_ps)
            pe.wait_ge(w_split, 2)
            pe.wait_ge(xt_done, 1)
            project_qk(0)
            project_v(0)
            pe.wait_ge(consts, 2)
            for s in range(2):
                pe.wait_ge(qk_done, s + 1)
                pe.wait_ge(v_done, s + 1)
                project_qk(s + 1)
                project_v(s + 1)
                scores(s, s)
            with pe.Fori(0, B) as i:
                for hp in range(HP):
                    s = i * HP + hp
                    pe.wait_ge(prob_done, s * 2 + 2)
                    for h in range(2):
                        for t in range(3):
                            last = nc.tensor.transpose(PT[:, h, t * P:(t + 1) * P],
                                                       prob[:, hp % 2, h, t * P:(t + 1) * P], g.ident[:])
                    last.then_inc(pt_ps, 1)
                    pe.wait_ge(qk_done, s + 3)
                    scores(hp % 2, hp + 2)
                    if hp == 2:
                        pe.wait_ge(nrm_done, i + 1)
                        rows_to_columns(nrm, ntr_ps)
                    if hp == 5:
                        pe.wait_ge(x_in, i * 16 + 32)
                        rows_to_columns(xin, xtr_ps)
                    if hp == 0:
                        output(i * HP + 1, y_ps)
                    pe.wait_ge(v_done, s + 3)
                    pe.wait_ge(pt_done, s + 1)
                    for h in range(2):
                        out = VO[h * DK0:(h + 1) * DK0, :]
                        at = slice(h * DK0, (h + 1) * DK0)
                        nc.tensor.matmul(out[:, 0:T], v[:, hp % 4, 0, at], probt[:, hp % 2, h, 0:T], start=True, stop=False)
                    for h in range(2):
                        out = VO[h * DK0:(h + 1) * DK0, :]
                        at = slice(h * DK0, (h + 1) * DK0)
                        last = nc.tensor.matmul(out[:, P:T], v[:, hp % 4, 1, at], probt[:, hp % 2, h, T:SW],
                                                start=False, stop=True)
                    last.then_inc(pv_ps, 1)
                    if hp == 0:
                        pe.wait_ge(res_done, i + 1)
                    if hp == 2:
                        pe.wait_ge(nt_done, i + 1)
                    if hp == 5:
                        pe.wait_ge(xt_done, i + 2)
                    project_qk(hp + 3)
                    pe.wait_ge(ot_done, s + 2)
                    project_v(hp + 3)
            pe.wait_ge(qk_done, B * HP + 3)
            output(B * HP + 1, y_ps)
            pe.wait_ge(nrm_done, B + 1)
            rows_to_columns(nrm, ntr_ps)


def moe(nc, ctx, g, d, tag, gated):
    sb = lambda name, shape, dt=F32: ctx.enter_context(nc.sbuf_tensor(tag + name, shape, dt))
    sem = lambda name: ctx.enter_context(nc.semaphore(tag + name))
    FB = FB0 if gated else FB1
    U = (E0 if gated else E1 + S1) * FB
    WC = W0C if gated else W1C
    UP0 = F0 if gated else 0
    DN0 = 2 * F0 if gated else F1
    E = E0
    spread_at = [8 + (3 if gated else 1) * e for e in range(E)]
    D = 2 if gated else 4
    LAG = D // 2
    ROUTED = E * FB
    on_act = lambda w: gated or w % 4 != 3
    ON_ACT = sum(map(on_act, range(U)))
    leaves = lambda w: max(w - D + 1, 1) if w >= LAG else w - D + 1

    rw32 = sb("rw32", [P, P])
    rw_h, rw_l = sb("rw_h", [P, P], F32R), sb("rw_l", [P, P], F32R)
    ident_r = sb("ident_r", [P, P], F32R)
    rb = sb("rb", [P, 1])
    iota = sb("iota", [P, E])
    ROWS = HOT_ROWS
    hot32 = sb("hot32", [ROWS, E, P])
    hot = sb("hot", [ROWS, E, P], F32R)
    logit = sb("logit", [P, GT])
    lt = sb("lt", [P, GB, E])
    top = sb("top", [P, GB, 8])
    topi = sb("topi", [P, GB, 8], U32)
    topf = sb("topf", [P, GB, 2])
    gap = sb("gap", [P, GB])
    th = sb("th", [P, GB])
    pr = sb("pr", [P, 2, GB])
    comb2 = sb("comb2", [P, 2, GB, E])
    comb = sb("comb", [P, GB, P])
    cb = sb("cb", [ROWS, GT], F32R)
    wb = sb("wb", [P, E, GT])
    act_out = sb("act_out", [P, 2, GT])
    hid = sb("hid", [P, D, GT])
    hid_h, hid_l = sb("hid_h", [P, D, GT], F32R), sb("hid_l", [P, D, GT], F32R)
    if gated:
        x32, xw32 = sb("x32", [P, GT]), sb("xw32", [P, GT])
        xw_h, xw_l = sb("xw_h", [P, 2, GT], F32R), sb("xw_l", [P, 2, GT], F32R)
        one = sb("one", [P, 1])
    rt = sb("rt", [P, GT])
    stats, mv = sb("stats", [P, GB, 6]), sb("mv", [P, GB, 2])
    veps, rstd, halfs = sb("veps", [P, GB]), sb("rstd", [P, GB]), sb("halfs", [P, GB])
    nrm = sb("nrm", [P, GB, P])
    if not gated:
        b1 = sb("b1", [P, U])
        b2_32 = sb("b2_32", [ROWS, P])
        b2_h, b2_l = sb("b2_h", [ROWS, P], F32R), sb("b2_l", [ROWS, P], F32R)
        sb2 = sb("sb2", [P, S1])
        sb2m = sb("sb2m", [P, 2])
    G, UP, Y = g.psum[:, 0:D, :], g.psum[:, 2:4, :], g.psum[:, 4, :]
    R, WB, N = g.psum[:, 5, :], g.psum[:, 6, :], g.psum[:, 7, :]

    loaded, consts, hot_done, dve_chain = sem("loaded"), sem("consts"), sem("hot_done"), sem("dve_chain")
    up_ps, act_done, prod_done, hi_done, hid_done, down_ps, xw_done, pool_chain = (sem(n) for n in (
        "up_ps", "act_done", "prod_done", "hi_done", "hid_done", "down_ps", "xw_done", "pool_chain"))
    y_ps, rt_done, rows_ps, var_done, rstd_done, nrm_done, ntr_ps, nt_act, rows_free = (sem(n) for n in (
        "y_ps", "rt_done", "rows_ps", "var_done", "rstd_done", "nrm_done", "ntr_ps", "nt_act", "rows_free"))
    logit_ps, logit_done, lt_ps, gap_done, th_done, comb_done, ct_ps, cb_done, wb_ps, wb_done = (sem(n) for n in (
        "logit_ps", "logit_done", "lt_ps", "gap_done", "th_done", "comb_done", "ct_ps", "cb_done", "wb_ps", "wb_done"))
    stored = sem("stored")
    LOADS = 5 if gated else 8

    with nc.Block() as block:
        @block.sync
        def _(sp):
            names = [(rw32, "rw"), (rb, "rb"), (iota, "iota"), (hot32, "hot")] + (
                [] if gated else [(b1, "b1"), (b2_32, "b2"), (sb2, "sb2")])
            for tile, name in names:
                sp.dma_start(tile[:], d[tag + name] if name not in ("iota", "hot") else d[name]).then_inc(loaded, 16)
            sp.dma_start(rt[:], d["zeros"]).then_inc(loaded, 16)
            if not gated:
                sp.sem_inc(stored, 16)
                with sp.Fori(0, NG) as n:
                    sp.wait_ge(nrm_done, n + 1)
                    sp.dma_start(d["out"][bass.ds(n * GT, GT)].rearrange("(b p) f -> p b f", p=P), nrm[:]
                                 ).then_inc(stored, 16)
                sp.wait_ge(nrm_done, NG + 1)
                sp.dma_start(d["out"][NG * GT:(NG + 1) * GT].rearrange("(b p) f -> p b f", p=P), nrm[:]
                             ).then_inc(stored, 16)
                sp.wait_ge(stored, 16 * (NG + 2))

        @block.tensor
        def _(pe):
            def project(w, at, n, xw_n):
                e, f = w // FB, w % FB
                c = slice(e * WC + f * P, e * WC + (f + 1) * P)
                if n is not None:
                    pe.wait_ge(prod_done if gated else act_done, n)
                last = split_mm(nc, G[:, w % D, :], g.wh[:, c], g.wl[:, c], g.xth[:, at], g.xtl[:, at], True, True)
                if gated:
                    c = slice(e * WC + UP0 + f * P, e * WC + UP0 + (f + 1) * P)
                    if f == 0:
                        pe.wait_ge(xw_done, xw_n)
                    last = split_mm(nc, UP[:, w % 2, :], g.wh[:, c], g.wl[:, c], xw_h[:, e % 2, :], xw_l[:, e % 2, :],
                                    True, True)
                last.then_inc(up_ps, 1)

            def down(u):
                e, f = u // FB, u % FB
                c = slice(e * WC + DN0 + f * P, e * WC + DN0 + (f + 1) * P)
                split_mm(nc, Y, g.wh[:, c], g.wl[:, c], hid_h[:, u % D, :], hid_l[:, u % D, :],
                         u == 0, u == U - 1).then_inc(down_ps, 1)

            def router_logits(at, n):
                pe.wait_ge(cb_done, n)
                split_mm(nc, R, rw_h[:], rw_l[:], g.xth[:, at], g.xtl[:, at], True, True).then_inc(logit_ps, 1)

            def router_rows(n):
                pe.wait_ge(logit_done, n)
                for b in range(GB):
                    last = nc.tensor.transpose(R[:, b * P:(b + 1) * P], logit[:, b * P:(b + 1) * P], g.ident[:])
                last.then_inc(lt_ps, 1)

            def router_columns(n):
                pe.wait_ge(comb_done, n)
                for b in range(GB):
                    last = nc.tensor.transpose(R[:, b * P:(b + 1) * P], comb[:, b, :], g.ident[:])
                last.then_inc(ct_ps, 1)

            def spread(e, n):
                pe.wait_ge(cb_done, n)
                if not isinstance(n, int):
                    pe.wait_ge(wb_done, (n - 1) * E + e)
                elif e >= 2:
                    pe.wait_ge(wb_done, e - 1)
                nc.tensor.matmul(N if isinstance(n, int) and e % 2 else WB, hot[:, e, :], cb[:], start=True, stop=True).then_inc(wb_ps, 1)

            def rows(n):
                pe.wait_ge(rt_done, n)
                pe.wait_ge(rows_free, n)
                for b in range(GB):
                    last = nc.tensor.transpose(N[:, b * P:(b + 1) * P], rt[:, b * P:(b + 1) * P], g.ident[:])
                last.then_inc(rows_ps, 1)

            def columns(n):
                pe.wait_ge(nrm_done, n)
                for b in range(GB):
                    last = nc.tensor.transpose(N[:, b * P:(b + 1) * P], nrm[:, b, :], g.ident[:])
                last.then_inc(ntr_ps, 1)

            pe.wait_ge(loaded, LOADS * 16)
            first = slice(PAD, PAD + GT)
            pe.wait_ge(consts, 2)
            split_mm(nc, R, rw_h[:], rw_l[:], g.xth[:, first], g.xtl[:, first], True, True).then_inc(logit_ps, 1)
            router_rows(1)
            router_columns(1)
            pe.wait_ge(hot_done, 1)
            for e in range(E):
                spread(e, 1)
            for w in range(D):
                project(w, first, None, 1)
            pe.wait_ge(wb_done, E)
            with pe.Fori(0, NG) as n:
                here, ahead = bass.ds(n * GT + PAD, GT), bass.ds(n * GT + (PAD + GT), GT)
                for u in range(U):
                    w = u + D
                    project(w % U, here if w < U else ahead, n * U + u + 1, n * E + w // FB + 1)
                    if u == 0:
                        router_logits(ahead, n + 1)
                    if u == 1:
                        rows(n + 1)
                    if u == 2:
                        router_rows(n + 2)
                    if u == 5 and gated:
                        columns(n + 1)
                    if u == 6:
                        router_columns(n + 2)
                    pe.wait_ge(hid_done, n * U + u + 1)
                    if u == 0:
                        pe.wait_ge(rt_done, n + 1)
                    down(u)
                    if u == 0:
                        nc.tensor.matmul(Y, ident_r[:], g.xth[:, here], start=False, stop=False)
                        nc.tensor.matmul(Y, ident_r[:], g.xtl[:, here], start=False, stop=False)
                        if not gated:
                            nc.tensor.matmul(Y, b2_h[:], cb[:], start=False, stop=False)
                            nc.tensor.matmul(Y, b2_l[0:E], cb[0:E], start=False, stop=False)
                    for e in range(E):
                        if spread_at[e] == u:
                            spread(e, n + 2)
            rows(NG + 1)
            if gated:
                columns(NG + 1)

        @block.scalar
        def _(act):
            def activate(w, k):
                act.wait_ge(up_ps, k * U + w + 1)
                looped = not isinstance(k, int)
                if gated:
                    if looped:
                        act.wait_ge(prod_done, k * U + w - 1)
                    last = nc.scalar.activation(act_out[:, w % 2, :], G[:, w % D, :], ACT.Silu)
                elif w < ROUTED:
                    if looped or w >= 2:
                        act.wait_ge(prod_done, k * ROUTED + w - 1)
                    last = nc.scalar.activation(act_out[:, w % 2, :], G[:, w % D, :], ACT.Gelu, bias=b1[:, w:w + 1])
                else:
                    act.wait_ge(hid_done, k * U + w - D + 1)
                    last = nc.scalar.activation(hid[:, w % D, :], G[:, w % D, :], ACT.Gelu, bias=b1[:, w:w + 1])
                last.then_inc(act_done, 1)

            def high(w, k):
                if w < ROUTED:
                    act.wait_ge(prod_done, k * ROUTED + w + 1)
                else:
                    act.wait_ge(act_done, k * U + w + 1)
                if not isinstance(k, int):
                    act.wait_ge(down_ps, k * U + leaves(w))
                nc.scalar.activation(hid_h[:, w % D, :], hid[:, w % D, :], ACT.Copy).then_inc(hi_done, 1)

            def tanh(n):
                act.wait_ge(gap_done, n)
                nc.scalar.activation(th[:], gap[:], ACT.Tanh, scale=0.5).then_inc(th_done, 1)

            def spread(e, n, used):
                act.wait_ge(wb_ps, (n - 1) * E + e + 1)
                if used is not None:
                    act.wait_ge(xw_done if gated else prod_done, used)
                nc.scalar.activation(wb[:, e, :], N if used is None and e % 2 else WB, ACT.Copy).then_inc(wb_done, 1)

            def residual(n):
                act.wait_ge(down_ps, n)
                if gated:
                    last = nc.scalar.activation(rt[:], Y, ACT.Copy)
                else:
                    last = nc.scalar.activation(rt[:], Y, ACT.Identity, bias=sb2m[:, 1:2])
                last.then_inc(rt_done, 1)

            def columns(at, n):
                act.wait_ge(ntr_ps, n)
                nc.scalar.activation(g.xth[:, at], N, ACT.Copy).then_inc(nt_act, 1)

            act.wait_ge(loaded, LOADS * 16)
            act.wait_ge(consts, 2)
            act.sem_inc(rt_done, 1)
            tanh(1)
            for e in range(E):
                spread(e, 1, None)
            for w in range(D):
                activate(w, 0)
            for w in range(LAG):
                high(w, 0)
            with act.Fori(0, NG) as n:
                for u in range(U):
                    for e in range(E):
                        if spread_at[e] + 1 == u:
                            spread(e, n + 2, n * E + e + 1 if gated else n * ROUTED + (e + 1) * FB)
                    if u == 4:
                        tanh(n + 2)
                    if u == 6 and gated:
                        columns(bass.ds(n * GT, GT), n + 1)
                    w = u + LAG
                    if on_act(w % U):
                        high(w % U, n + w // U)
                    w = u + D
                    activate(w % U, n + w // U)
                residual(n * U + U)
            if gated:
                columns(slice(NG * GT, (NG + 1) * GT), NG + 1)

        @block.gpsimd
        def _(pool):
            chain = Counter(pool, pool_chain)

            def gather_input(at):
                chain.done(nc.gpsimd.tensor_tensor(x32[:], g.xth[:, at].bitcast(F32), g.xtl[:, at].bitcast(F32), ALU.add))

            def weigh_input(e, k, free):
                pool.wait_ge(wb_done, k * E + e + 1)
                chain.done(nc.gpsimd.tensor_tensor(xw32[:], x32[:], wb[:, e, :], ALU.mult))
                if free is not None:
                    pool.wait_ge(up_ps, free)
                chain.done(nc.gpsimd.tensor_tensor(xw_h[:, e % 2, :], xw32[:], one[:].to_broadcast([P, GT]), ALU.mult))
                nc.gpsimd.tensor_tensor(xw_l[:, e % 2, :], xw32[:], xw_h[:, e % 2, :].bitcast(F32), ALU.subtract
                                        ).then_inc(xw_done, 1)
                pool.wait_ge(xw_done, k * E + e + 1)

            def weigh(w, k):
                pool.wait_ge(act_done, k * U + w + 1)
                if not isinstance(k, int):
                    pool.wait_ge(hid_done, k * U + w - D + 1)
                if w % FB == 0:
                    pool.wait_ge(wb_done, k * E + w // FB + 1)
                nc.gpsimd.tensor_tensor(hid[:, w % D, :], act_out[:, w % 2, :], wb[:, w // FB, :], ALU.mult
                                        ).then_inc(prod_done, 1)

            def power(n):
                pool.wait_ge(var_done, n)
                nc.gpsimd.tensor_tensor(rstd[:], veps[:], halfs[:], ALU.pow).then_inc(rstd_done, 1)

            if gated:
                nc.gpsimd.memset(one[:], 1.0)
            nc.gpsimd.memset(halfs[:], -0.5).then_inc(consts, 1)
            if gated:
                pool.wait_ge(consts, 2)
                gather_input(slice(PAD, PAD + GT))
                weigh_input(0, 0, None)
            else:
                for w in range(D):
                    weigh(w, 0)
            with pool.Fori(0, NG) as n:
                if gated:
                    chain.loop(n, 2 * E + 1)
                    for e in range(1, E):
                        weigh_input(e, n, n * U + max((e - 1) * FB, 1))
                        if e == 1:
                            power(n + 1)
                    gather_input(bass.ds(n * GT + (PAD + GT), GT))
                    weigh_input(0, n + 1, n * U + (E - 1) * FB)
                else:
                    for u in range(U):
                        if u == 3:
                            power(n + 1)
                        w = u + D
                        if w % U < ROUTED:
                            weigh(w % U, n + w // U)
            if gated:
                chain.end(NG)
            power(NG + 1)

        @block.vector
        def _(dve):
            chain = Counter(dve, dve_chain)

            def product(w, k):
                dve.wait_ge(act_done, k * U + w + 1)
                if not isinstance(k, int):
                    dve.wait_ge(hid_done, k * U + w - 1)
                nc.vector.tensor_tensor(hid[:, w % D, :], act_out[:, w % 2, :], UP[:, w % 2, :], ALU.mult
                                        ).then_inc(prod_done, 1)

            def low(w, k):
                if on_act(w):
                    dve.wait_ge(hi_done, k * ON_ACT + sum(map(on_act, range(w + 1))))
                else:
                    if w < ROUTED:
                        dve.wait_ge(prod_done, k * ROUTED + w + 1)
                    else:
                        dve.wait_ge(act_done, k * U + w + 1)
                    if not isinstance(k, int):
                        dve.wait_ge(down_ps, k * U + leaves(w))
                    chain.done(nc.vector.tensor_copy(hid_h[:, w % D, :], hid[:, w % D, :]))
                nc.vector.tensor_tensor(hid_l[:, w % D, :], hid[:, w % D, :], hid_h[:, w % D, :].bitcast(F32),
                                        ALU.subtract).then_inc(hid_done, 1)

            def router_logits(n):
                dve.wait_ge(logit_ps, n)
                nc.vector.tensor_scalar(logit[:], R, rb[:], None, ALU.add).then_inc(logit_done, 1)

            def router_top(n):
                dve.wait_ge(lt_ps, n)
                chain.done_apart(nc.vector.tensor_copy(lt[:], R.rearrange("p (b n) -> p b n", b=GB)[:, :, 0:E]), g.spare[:])
                for b in range(GB):
                    last = nc.vector.max(top[:, b, :], lt[:, b, :])
                chain.done_apart(last, g.spare[:])
                for b in range(GB):
                    last = nc.vector.max_index(topi[:, b, :], top[:, b, :], lt[:, b, :])
                chain.done(last)
                nc.vector.tensor_copy(topf[:], topi[:, :, 0:2])
                nc.vector.tensor_tensor(gap[:], top[:, :, 0], top[:, :, 1], ALU.subtract).then_inc(gap_done, 1)

            def router_weights(n):
                dve.wait_ge(th_done, n)
                nc.vector.tensor_scalar(pr[:, 0, :], th[:], 0.5, 0.5, ALU.mult, ALU.add)
                chain.done(nc.vector.tensor_scalar(pr[:, 1, :], th[:], -0.5, 0.5, ALU.mult, ALU.add))
                for k in range(2):
                    for b in range(GB):
                        last = nc.vector.tensor_scalar(comb2[:, k, b, :], iota[:], topf[:, b, k:k + 1], pr[:, k, b:b + 1],
                                                       ALU.is_equal, ALU.mult)
                chain.done(last)
                nc.vector.tensor_tensor(comb[:, :, 0:E], comb2[:, 0], comb2[:, 1], ALU.add)
                nc.vector.tensor_tensor(comb[:, :, LOW:ROWS], comb2[:, 0], comb2[:, 1], ALU.add).then_inc(comb_done, 1)

            def router_columns(n):
                dve.wait_ge(ct_ps, n)
                chain.done(nc.vector.tensor_copy(cb[:], R[0:ROWS, :]))
                nc.vector.tensor_tensor(cb[LOW:ROWS, :], R[LOW:ROWS, :], cb[LOW:ROWS, :].bitcast(F32), ALU.subtract
                                        ).then_inc(cb_done, 1)

            def variances(n):
                dve.wait_ge(rows_ps, n)
                for b in range(GB):
                    last = nc.vector.bn_stats(stats[:, b, :], N[:, b * P:(b + 1) * P])
                chain.done_apart(last, g.spare[:])
                for b in range(GB):
                    last = nc.vector.bn_aggr(mv[:, b, :], stats[:, b:b + 1, :])
                chain.done(last)
                nc.vector.tensor_scalar(veps[:], mv[:, :, 1], EPS, None, ALU.add).then_inc(var_done, 1)

            def normalise(n):
                dve.wait_ge(rstd_done, n)
                if not gated:
                    dve.wait_ge(stored, n * 16)
                for b in range(GB):
                    last = nc.vector.tensor_scalar(nrm[:, b, :], N[:, b * P:(b + 1) * P], mv[:, b, 0:1], rstd[:, b:b + 1],
                                                   ALU.subtract, ALU.mult)
                chain.done(last)
                dve.sem_inc(nrm_done, 1)
                if not gated:
                    dve.sem_inc(rows_free, 1)

            def columns(at, n):
                dve.wait_ge(nt_act, n)
                nc.vector.tensor_tensor(g.xtl[:, at], N, g.xth[:, at].bitcast(F32), ALU.subtract).then_inc(rows_free, 1)

            nc.vector.memset(comb[:], 0.0)
            dve.wait_ge(loaded, LOADS * 16)
            chain.done(nc.vector.tensor_copy(rw_h[:], rw32[:]))
            nc.vector.tensor_tensor(rw_l[:], rw32[:], rw_h[:].bitcast(F32), ALU.subtract).then_inc(consts, 1)
            nc.vector.tensor_copy(ident_r[:], g.ident[:])
            if not gated:
                nc.vector.tensor_copy(b2_h[:], b2_32[:])
                chain.done(nc.vector.tensor_tensor(sb2m[:, 0:1], sb2[:, 0:1], sb2[:, 1:2], ALU.add))
                nc.vector.tensor_tensor(b2_l[:], b2_32[:], b2_h[:].bitcast(F32), ALU.subtract)
                nc.vector.tensor_scalar(sb2m[:, 1:2], sb2m[:, 0:1], 1.0 / S1, None, ALU.mult)
            if not gated:
                for part in (g.wh, g.wl):
                    for e in range(E, E + S1):
                        c = part[:, e * WC + DN0:(e + 1) * WC]
                        nc.vector.tensor_scalar(c, c.bitcast(F32), 1.0 / S1, None, ALU.mult)
            nc.vector.tensor_copy(hot[:], hot32[:]).then_inc(hot_done, 1)
            dve.sem_inc(rows_free, 1)
            router_logits(1)
            router_top(1)
            router_weights(1)
            router_columns(1)
            if gated:
                product(0, 0)
            for w in range(LAG):
                low(w, 0)
            if gated:
                product(1, 0)
            with dve.Fori(0, NG) as n:
                chain.loop(n, U - ON_ACT + 9)
                for u in range(U):
                    if u == 1:
                        router_logits(n + 2)
                    if u == 2:
                        variances(n + 1)
                    if u == 3:
                        router_top(n + 2)
                    if u == 4:
                        normalise(n + 1)
                    if u == 5:
                        router_weights(n + 2)
                    if u == 6 and gated:
                        columns(bass.ds(n * GT, GT), n + 1)
                    if u == 7:
                        router_columns(n + 2)
                    w = u + LAG
                    low(w % U, n + w // U)
                    if gated:
                        w = u + D
                        product(w % U, n + w // U)
            chain.end(NG)
            variances(NG + 1)
            normalise(NG + 1)
            if gated:
                columns(slice(NG * GT, (NG + 1) * GT), NG + 1)


def attention1(nc, ctx, g, d):
    sb = lambda name, shape, dt=F32: ctx.enter_context(nc.sbuf_tensor("a1_" + name, shape, dt))
    sem = lambda name: ctx.enter_context(nc.semaphore("a1_" + name))
    SCALE = DH1 ** -0.5
    HG = 4
    NGR = H1 // HG
    NPR = H1 // 2
    VW = 32
    WS = (E1 + S1) * W1C // B
    BT = QB * P

    prob = sb("prob", [P, 2, HG, QB * T])
    sel = sb("sel", [P, 4, NGR, P], F32R)
    pick = sb("pick", [P, H1, P], F32R)
    rows = sb("rows", [P, H1])
    warm = sb("warm", [P, HG])
    small32 = sb("small32", [P, 3, P])
    rot = sb("rot", [P, P], F32R)
    ident_r = sb("ident_r", [P, P], F32R)
    wd_h, wd_l = sb("wd_h", [P, 2, P], F32R), sb("wd_l", [P, 2, P], F32R)
    wu = sb("wu", [P, 3, P])
    bias = sb("bias", [P, 4])
    buv = sb("buv", [P, P])
    cos, sin = sb("cos", [P, T]), sb("sin", [P, T])
    lat = sb("lat", [P, 2, T])
    k32, x32 = sb("k32", [P, T]), sb("x32", [P, T])
    xcos, kcos, xsin, ksin = (sb(n, [P, T]) for n in ("xcos", "kcos", "xsin", "ksin"))
    rq, rk = sb("rq", [P, T]), sb("rk", [P, T])
    qk_h, qk_l = sb("qk_h", [P, 2, T], F32R), sb("qk_l", [P, 2, T], F32R)
    q_stk = sb("q_stk", [P, 2, H1, T], F32R)
    k_stk = sb("k_stk", [P, 2, NGR, T], F32R)
    in_head = sb("in_head", [P, HG])
    v = sb("v", [P, 2, QB, H1, VW])
    mx = sb("mx", [P, QB, H1])
    mh = sb("mh", [P, QB, 2 * H1], F32R)
    nmx = sb("nmx", [P, QB, H1])
    mt = sb("mt", [P, T], F32R)
    osb = sb("osb", [P, NGR, T])
    rs = sb("rs", [P, QB, H1])
    o = sb("o", [P, QB, P])
    ot = sb("ot", [P, T])
    rt = sb("rt", [P, T])
    stats, mv = sb("stats", [P, QB, 6]), sb("mv", [P, QB, 2])
    veps, rstd, halfs = sb("veps", [P, QB]), sb("rstd", [P, QB]), sb("halfs", [P, QB])
    one = sb("one", [P, 1])
    nrm = sb("nrm", [P, QB, P])
    stage = sb("stage", [P, 2, WS])
    ST = g.psum[:, 0:4, :]
    R0, R1, PV, MISC = (g.psum[:, k, :] for k in (4, 5, 6, 7))

    loaded, consts, dve_chain, pool_chain = sem("loaded"), sem("consts"), sem("dve_chain"), sem("pool_chain")
    sel_in, sel_done = sem("sel_in"), sem("sel_done")
    lat_ps, lat_done, k_ps, k_done, v_ps, v_done = (sem(n) for n in (
        "lat_ps", "lat_done", "k_ps", "k_done", "v_ps", "v_done"))
    xsin_done, ksin_done, xcos_done, kcos_done, q_split, k_split = (sem(n) for n in (
        "xsin_done", "ksin_done", "xcos_done", "kcos_done", "q_split", "k_split"))
    stack_ps, stack_act, stack_dve, s1_ps, mx_done, nmx_done, mt_ps, mt_done = (sem(n) for n in (
        "stack_ps", "stack_act", "stack_dve", "s1_ps", "mx_done", "nmx_done", "mt_ps", "mt_done"))
    st_ps, exp_done, pv_ps, osb_done = (sem(n) for n in ("st_ps", "exp_done", "pv_ps", "osb_done"))
    o_ps, o_done, ot_ps, ot_done, y_ps, rt_done, rows_ps, var_done, rstd_done, nrm_done, ntr_ps, nt_act, nt_done = (
        sem(n) for n in ("o_ps", "o_done", "ot_ps", "ot_done", "y_ps", "rt_done", "rows_ps", "var_done", "rstd_done",
                         "nrm_done", "ntr_ps", "nt_act", "nt_done"))
    stage_in = [sem("stage_in0"), sem("stage_in1")]
    stage_free = sem("stage_free")
    LOADS = 9

    def columns_of(n):
        return bass.ds(n * T + PAD, T)

    with nc.Block() as block:
        @block.sync
        def _(sp):
            for dst, src in ((small32[:], d["small"]),
                             (wu[:, 0, :], d["w_uk"]), (wu[:, 1, :], d["w_uv"]), (wu[:, 2, :], d["w_o"]),
                             (bias[:], d["a1_bias"]), (buv[:], d["b_uv"].partition_broadcast(P)),
                             (cos[:], d["cos"]), (sin[:], d["sin"]), (in_head[:], d["in_head"])):
                sp.dma_start(dst, src).then_inc(loaded, 16)
            sp.dma_start(prob[:].rearrange("p a h t -> p (a h t)")[:, 0:H1 * P], d["sel"]).then_inc(sel_in, 16)
            with sp.Fori(0, B // 2) as j:
                for half in range(2):
                    n = j * 2 + half
                    sp.wait_ge(stage_free, n + 1)
                    sp.dma_start(stage[:, half, :], d["w1"][:, bass.ds(n * WS, WS)]).then_inc(stage_in[half], 16)

        @block.tensor
        def _(pe):
            def latents(at, n):
                for j in range(2):
                    last = split_mm(nc, MISC[:, j * T:(j + 1) * T], wd_h[:, j, :], wd_l[:, j, :], g.xth[:, at],
                                    g.xtl[:, at], True, True)
                last.then_inc(lat_ps, 1)

            def keys(at, n):
                pe.wait_ge(lat_done, n)
                nc.tensor.matmul(MISC[:, 0:T], wu[:, 0, :], lat[:, 0, :], start=True, stop=True)
                nc.tensor.matmul(MISC[:, T:2 * T], rot[:], g.xth[:, at], start=True, stop=False)
                nc.tensor.matmul(MISC[:, T:2 * T], rot[:], g.xtl[:, at], start=False, stop=True).then_inc(k_ps, 1)

            def values(n):
                pe.wait_ge(k_done, n)
                pe.wait_ge(xsin_done, n)
                for q in range(QB):
                    nc.tensor.matmul(MISC[:, q * P:(q + 1) * P], lat[:, 1, q * P:(q + 1) * P], wu[:, 1, :],
                                     start=True, stop=True)
                nc.tensor.matmul(MISC[:, T:2 * T], small32[:, 2, :], k32[:], start=True, stop=True).then_inc(v_ps, 1)

            def stacks(groups, n):
                pe.wait_ge(q_split, n)
                pe.wait_ge(k_split, n)
                for k in groups:
                    if k >= 2:
                        pe.wait_ge((stack_act, stack_dve)[k % 2], n * 2 - 1)
                    for j in range(2):
                        out = (R0, R1)[k % 2][:, j * T:(j + 1) * T]
                        nc.tensor.matmul(out, sel[:, 2 * j, k, :], qk_h[:, j, :], start=True, stop=False)
                        last = nc.tensor.matmul(out, sel[:, 2 * j + 1, k, :], qk_l[:, j, :], start=False, stop=True)
                    last.then_inc(stack_ps, 1)

            def first_scores(h, p, n):
                if h == 0:
                    pe.wait_ge(stack_act, n * 2)
                    pe.wait_ge(stack_dve, n * 2)
                if h >= 2:
                    pe.wait_ge(mx_done, n * H1 + (h - 1 - H1))
                for q in range(QB):
                    last = nc.tensor.matmul((R0, R1)[h % 2][:, q * T:(q + 1) * T], q_stk[:, p, h, q * P:(q + 1) * P],
                                            k_stk[:, p, h // HG, :], start=True, stop=True)
                last.then_inc(s1_ps, 1)

            def maxima(n):
                pe.wait_ge(nmx_done, n)
                for q in range(QB):
                    last = nc.tensor.transpose(R0[0:2 * H1, q * P:(q + 1) * P], mh[:, q, :].bitcast(F32), g.ident[:])
                last.then_inc(mt_ps, 1)

            def scores(t, p):
                for h in (2 * t, 2 * t + 1):
                    for k in range(QB):
                        out = ST[:, 2 * (t % 2) + h % 2, k * T:(k + 1) * T]
                        nc.tensor.matmul(out, k_stk[:, p, h // HG, k * P:(k + 1) * P], q_stk[:, p, h, :],
                                         start=True, stop=False)
                        last = nc.tensor.matmul(out, pick[:, h, :], mt[:], start=False, stop=True)
                last.then_inc(st_ps, 1)

            def outputs(k, p, n):
                pe.wait_ge(exp_done, n * NPR + 2 * k + 2)
                pe.wait_ge(osb_done, n * NGR + k + 1)
                for b in range(QB):
                    for j in range(HG):
                        rows = slice(32 * j, 32 * j + 32)
                        last = nc.tensor.matmul(PV[rows, (k % 2) * T:(k % 2 + 1) * T], v[:, p, b, HG * k + j, :],
                                                prob[:, k % 2, j, b * T:(b + 1) * T], start=b == 0, stop=b == QB - 1,
                                                tile_position=(0, 32 * j))
                last.then_inc(pv_ps, 1)

            def tail_heads(n):
                pe.wait_ge(osb_done, n * NGR - (NGR - 1))
                for q in range(QB):
                    for k in range(NGR):
                        last = nc.tensor.transpose((R0, R1)[q][:, k * P:(k + 1) * P], osb[:, k, q * P:(q + 1) * P], g.ident[:])
                last.then_inc(o_ps, 1)

            def tail_columns(n):
                pe.wait_ge(o_done, n)
                for q in range(QB):
                    last = nc.tensor.transpose(R0[:, q * P:(q + 1) * P], o[:, q, :], g.ident[:])
                last.then_inc(ot_ps, 1)

            def tail_project(at, n):
                pe.wait_ge(ot_done, n)
                out = R1[:, 0:T]
                nc.tensor.matmul(out, wu[:, 2, :], ot[:], start=True, stop=False)
                nc.tensor.matmul(out, ident_r[:], g.xth[:, at], start=False, stop=False)
                nc.tensor.matmul(out, ident_r[:], g.xtl[:, at], start=False, stop=True).then_inc(y_ps, 1)

            def tail_rows(n):
                pe.wait_ge(rt_done, n)
                for q in range(QB):
                    last = nc.tensor.transpose(MISC[:, q * P:(q + 1) * P], rt[:, q * P:(q + 1) * P], g.ident[:])
                last.then_inc(rows_ps, 1)

            def tail_store(n):
                pe.wait_ge(nrm_done, n)
                for q in range(QB):
                    last = nc.tensor.transpose(MISC[:, q * P:(q + 1) * P], nrm[:, q, :], g.ident[:])
                last.then_inc(ntr_ps, 1)

            pe.wait_ge(loaded, LOADS * 16)
            pe.wait_ge(consts, 2)
            at = columns_of(0)
            latents(at, 1)
            keys(at, 1)
            values(1)
            pe.wait_ge(sel_done, 1)
            stacks(range(NGR), 1)
            for h in range(H1):
                first_scores(h, 0, 1)
            pe.wait_ge(v_done, 1)
            pe.wait_ge(ksin_done, 1)
            latents(columns_of(1), 2)
            maxima(1)
            keys(columns_of(1), 2)
            with pe.Fori(0, B // 2) as i:
                for p in range(2):
                    n = i * 2 + p
                    ahead, behind = columns_of(n + 2), columns_of(n - 1)
                    for t in range(NPR):
                        if t == 0:
                            pe.wait_ge(mt_done, n + 1)
                            pe.wait_ge(v_done, n + 1)
                        if t >= 2:
                            pe.wait_ge(exp_done, n * NPR + t - 1)
                        if t >= 5:
                            for h in range(4 * t - 16, 4 * t - 14):
                                first_scores(h, 1 - p, n + 2)
                        scores(t, p)
                        if t == 2:
                            tail_project(behind, n + 1)
                            pe.wait_ge(rt_done, n + 1)
                            stacks((0, 1), n + 2)
                        if t == 4:
                            outputs(1, p, n)
                        if t >= 4:
                            for h in range(4 * t - (16 if t == 4 else 14), 4 * t - 12):
                                first_scores(h, 1 - p, n + 2)
                        if t in (2, 6):
                            outputs(t // 2 - 1, p, n)
                        if t == 0:
                            tail_heads(n + 1)
                        if t == 1:
                            values(n + 2)
                            tail_columns(n + 1)
                        if t == 3:
                            pe.wait_ge(v_done, n + 2)
                            pe.wait_ge(ksin_done, n + 2)
                            stacks((2, 3), n + 2)
                            tail_rows(n + 1)
                        if t == 5:
                            tail_store(n + 1)
                    pe.wait_ge(nt_done, n + 1)
                    latents(ahead, n + 3)
                    maxima(n + 2)
                    keys(ahead, n + 3)
                    outputs(NGR - 1, p, n)
            pe.wait_ge(mt_done, B + 1)
            pe.wait_ge(k_done, B + 2)
            tail_heads(B + 1)
            tail_columns(B + 1)
            tail_project(columns_of(B - 1), B + 1)
            tail_rows(B + 1)
            tail_store(B + 1)

        @block.scalar
        def _(act):
            def latents(n):
                act.wait_ge(lat_ps, n)
                for j in range(2):
                    last = nc.scalar.activation(lat[:, j, :], MISC[:, j * T:(j + 1) * T], ACT.Identity, bias=bias[:, j:j + 1])
                last.then_inc(lat_done, 1)

            def keys(n):
                act.wait_ge(k_ps, n)
                nc.scalar.activation(k32[:], MISC[:, 0:T], ACT.Identity, bias=bias[:, 2:3]).then_inc(k_done, 1)

            def stacks(k, p, n):
                act.wait_ge(stack_ps, n * NGR + (k + 1 - NGR))
                for j in range(HG):
                    nc.scalar.activation(q_stk[:, p, k * HG + j, :], R0[:, 0:T], ACT.Identity, scale=in_head[:, j:j + 1])
                nc.scalar.activation(k_stk[:, p, k, :], R0[:, T:2 * T], ACT.Copy).then_inc(stack_act, 1)

            def exps(t, n):
                act.wait_ge(st_ps, n * NPR + t + 1)
                k = t // 2
                nc.scalar.activation(prob[:, k % 2, 2 * (t % 2):2 * (t % 2) + 2, :], ST[:, 2 * (t % 2):2 * (t % 2) + 2, :],
                                     ACT.Exp, scale=SCALE).then_inc(exp_done, 1)

            def outputs(k, n):
                act.wait_ge(pv_ps, n * NGR + k + 1)
                nc.scalar.activation(osb[:, k, :], PV[:, (k % 2) * T:(k % 2 + 1) * T], ACT.Copy).then_inc(osb_done, 1)

            def tail_columns(n):
                act.wait_ge(ot_ps, n)
                nc.scalar.activation(ot[:], R0[:, 0:T], ACT.Copy).then_inc(ot_done, 1)

            def tail_residual(n):
                act.wait_ge(y_ps, n)
                nc.scalar.activation(rt[:], R1[:, 0:T], ACT.Identity, bias=bias[:, 3:4]).then_inc(rt_done, 1)

            def tail_store(at, n):
                act.wait_ge(ntr_ps, n)
                nc.scalar.activation(g.xth[:, at], MISC[:, 0:T], ACT.Copy).then_inc(nt_act, 1)

            act.wait_ge(loaded, LOADS * 16)
            act.wait_ge(consts, 2)
            nc.scalar.activation(warm[:], in_head[:], ACT.Exp)
            latents(1)
            keys(1)
            stacks(0, 0, 1)
            stacks(2, 0, 1)
            latents(2)
            keys(2)
            with act.Fori(0, B // 2) as i:
                for p in range(2):
                    n = i * 2 + p
                    for t in range(NPR):
                        exps(t, n)
                        if t == 1:
                            tail_columns(n + 1)
                        if t == 2:
                            tail_residual(n + 1)
                            stacks(0, 1 - p, n + 2)
                        if t in (2, 4, 6):
                            outputs(t // 2 - 1, n)
                        if t == 3:
                            stacks(2, 1 - p, n + 2)
                        if t == 6:
                            tail_store(columns_of(n - 1), n + 1)
                    latents(n + 3)
                    keys(n + 3)
                    outputs(NGR - 1, n)
            tail_columns(B + 1)
            tail_residual(B + 1)
            tail_store(columns_of(B - 1), B + 1)

        @block.gpsimd
        def _(pool):
            def rotate_x(at, n, count):
                if not isinstance(n, int):
                    pool.wait_ge(q_split, n - 1)
                nc.gpsimd.tensor_tensor(x32[:], g.xth[:, at].bitcast(F32), g.xtl[:, at].bitcast(F32), ALU.add
                                        ).then_inc(pool_chain, 1)
                pool.wait_ge(pool_chain, count)
                nc.gpsimd.tensor_tensor(xcos[:], x32[:], cos[:], ALU.mult).then_inc(xcos_done, 1)

            def rotate_k(n):
                pool.wait_ge(k_done, n)
                if not isinstance(n, int):
                    pool.wait_ge(k_split, n - 1)
                nc.gpsimd.tensor_tensor(kcos[:], k32[:], cos[:], ALU.mult).then_inc(kcos_done, 1)

            def power(n):
                pool.wait_ge(var_done, n)
                nc.gpsimd.tensor_tensor(rstd[:], veps[:], halfs[:], ALU.pow).then_inc(rstd_done, 1)

            nc.gpsimd.memset(one[:], 1.0)
            nc.gpsimd.memset(halfs[:], -0.5).then_inc(consts, 1)
            pool.sem_inc(stage_free, 2)
            pool.wait_ge(loaded, LOADS * 16)
            rotate_x(columns_of(0), 1, 1)
            rotate_k(1)
            with pool.Fori(0, B // 2) as i:
                for half in range(2):
                    n = i * 2 + half
                    rotate_x(columns_of(n + 1), n + 2, n * 2 + 2)
                    rotate_k(n + 2)
                    power(n + 1)
                    at = bass.ds(n * WS, WS)
                    pool.wait_ge(stage_in[half], (i + 1) * 16)
                    nc.gpsimd.tensor_tensor(g.wh[:, at], stage[:, half, :], one[:].to_broadcast(stage[:, half, :].shape), ALU.mult).then_inc(pool_chain, 1)
                    pool.wait_ge(pool_chain, n * 2 + 3)
                    nc.gpsimd.tensor_tensor(g.wl[:, at], stage[:, half, :], g.wh[:, at].bitcast(F32),
                                            ALU.subtract).then_inc(stage_free, 1)
            power(B + 1)

        @block.vector
        def _(dve):
            chain = Counter(dve, dve_chain)

            def rotate(j, turned, sine, cosine, total, signal, n):
                chain.done(nc.vector.tensor_tensor(sine[:], turned, sin[:], ALU.mult))
                dve.sem_inc(signal[0], 1)
                dve.wait_ge(signal[1], n)
                chain.done(nc.vector.tensor_tensor(total[:], sine[:], cosine[:], ALU.add))
                chain.done(nc.vector.tensor_copy(qk_h[:, j, :], total[:]))
                nc.vector.tensor_tensor(qk_l[:, j, :], total[:], qk_h[:, j, :].bitcast(F32), ALU.subtract
                                        ).then_inc(signal[2], 1)

            def rotate_q(n):
                dve.wait_ge(k_done, n)
                rotate(0, MISC[:, T:2 * T], xsin, xcos, rq, (xsin_done, xcos_done, q_split), n)

            def values(p, n):
                dve.wait_ge(v_ps, n)
                nc.vector.tensor_tensor(v[:, p, :, :, 0:DH1], MISC[:, 0:BT].rearrange("p (q h e) -> p q h e", q=QB, h=H1),
                                        buv[:].rearrange("p (a h e) -> p a h e", a=1, h=H1).to_broadcast([P, QB, H1, DH1]),
                                        ALU.add).then_inc(v_done, 1)
                rotate(1, MISC[:, T:2 * T], ksin, kcos, rk, (ksin_done, kcos_done, k_split), n)

            def stacks(k, p, n):
                dve.wait_ge(stack_ps, n * NGR + (k + 1 - NGR))
                for j in range(HG):
                    nc.vector.tensor_scalar(q_stk[:, p, k * HG + j, :], R1[:, 0:T], in_head[:, j:j + 1], None, ALU.mult)
                nc.vector.tensor_copy(k_stk[:, p, k, :], R1[:, T:2 * T]).then_inc(stack_dve, 1)

            def maxima(h, n):
                dve.wait_ge(s1_ps, n * H1 + (h + 1 - H1))
                nc.vector.reduce_max(mx[:, :, h:h + 1], (R0, R1)[h % 2].rearrange("p (q k) -> p q k", q=QB), AX.X
                                     ).then_inc(mx_done, 1)

            def negate(n):
                dve.wait_ge(mx_done, n * H1)
                nc.vector.tensor_scalar(mh[:, :, 0:H1], mx[:], -1.0, None, ALU.mult)
                chain.done(nc.vector.tensor_scalar(nmx[:], mx[:], -1.0, None, ALU.mult))
                nc.vector.tensor_tensor(mh[:, :, H1:2 * H1], nmx[:], mh[:, :, 0:H1].bitcast(F32), ALU.subtract
                                        ).then_inc(nmx_done, 1)
                dve.wait_ge(mt_ps, n)
                nc.vector.tensor_copy(mt[0:2 * H1, :], R0[0:2 * H1, 0:T]).then_inc(mt_done, 1)

            def tail_heads(n):
                dve.wait_ge(o_ps, n)
                by_head = [r.rearrange("p (h e) -> p h e", h=H1) for r in (R0, R1)]
                for q in range(QB):
                    last = nc.vector.reciprocal(rs[:, q, :], by_head[q][:, :, DH1])
                chain.done(last)
                for q in range(QB):
                    last = nc.vector.tensor_tensor(o[:, q, :].rearrange("p (h e) -> p h e", h=H1), by_head[q][:, :, 0:DH1],
                                                   rs[:, q, :].rearrange("p (h a) -> p h a", a=1).to_broadcast([P, H1, DH1]),
                                                   ALU.mult)
                last.then_inc(o_done, 1)

            def variances(n):
                dve.wait_ge(rows_ps, n)
                for q in range(QB):
                    last = nc.vector.bn_stats(stats[:, q, :], MISC[:, q * P:(q + 1) * P])
                chain.done_apart(last, g.spare[:])
                for q in range(QB):
                    last = nc.vector.bn_aggr(mv[:, q, :], stats[:, q:q + 1, :])
                chain.done(last)
                nc.vector.tensor_scalar(veps[:], mv[:, :, 1], EPS, None, ALU.add).then_inc(var_done, 1)

            def normalise(n):
                dve.wait_ge(rstd_done, n)
                for q in range(QB):
                    last = nc.vector.tensor_scalar(nrm[:, q, :], MISC[:, q * P:(q + 1) * P], mv[:, q, 0:1], rstd[:, q:q + 1],
                                                   ALU.subtract, ALU.mult)
                last.then_inc(nrm_done, 1)

            def tail_store(at, n):
                dve.wait_ge(nt_act, n)
                nc.vector.tensor_tensor(g.xtl[:, at], MISC[:, 0:T], g.xth[:, at].bitcast(F32), ALU.subtract
                                        ).then_inc(nt_done, 1)

            nc.vector.tensor_tensor(rows[:], g.ident[:, 0:H1], g.ident[:, H1:2 * H1], ALU.add)
            chain.done(nc.vector.memset(v[:], 0.0))
            nc.vector.tensor_copy(pick[:], rows[:].rearrange("p (h a) -> p h a", a=1).to_broadcast([P, H1, P]))
            nc.vector.memset(v[:, :, :, :, DH1:DH1 + 1], 1.0)
            nc.vector.memset(osb[:], 1.0)
            nc.vector.memset(mt[:].bitcast(F32), 0.0).then_inc(osb_done, 1)
            dve.wait_ge(loaded, LOADS * 16)
            nc.vector.tensor_copy(wd_h[:], small32[:, 0:2, :])
            nc.vector.tensor_copy(ident_r[:], g.ident[:])
            chain.done(nc.vector.tensor_copy(rot[:], small32[:, 2, :]))
            nc.vector.tensor_tensor(wd_l[:], small32[:, 0:2, :], wd_h[:].bitcast(F32), ALU.subtract).then_inc(consts, 1)
            dve.wait_ge(sel_in, 16)
            nc.vector.tensor_copy(sel[:].rearrange("p a k n -> p (a k n)"),
                                  prob[:].rearrange("p a h t -> p (a h t)")[:, 0:H1 * P]).then_inc(sel_done, 1)
            rotate_q(1)
            values(0, 1)
            stacks(1, 0, 1)
            stacks(3, 0, 1)
            for h in range(H1):
                maxima(h, 1)
            negate(1)
            with dve.Fori(0, B // 2) as i:
                chain.loop(i, 2 * 10)
                for p in range(2):
                    n = i * 2 + p
                    rotate_q(n + 2)
                    tail_heads(n + 1)
                    values(1 - p, n + 2)
                    stacks(1, 1 - p, n + 2)
                    stacks(3, 1 - p, n + 2)
                    variances(n + 1)
                    for t in range(4, NPR):
                        for h in range(4 * (t - 4), 4 * (t - 3)):
                            maxima(h, n + 2)
                        if t == 4:
                            normalise(n + 1)
                        if t == 6:
                            tail_store(columns_of(n - 1), n + 1)
                    negate(n + 2)
            chain.end(B // 2)
            tail_heads(B + 1)
            variances(B + 1)
            normalise(B + 1)
            tail_store(columns_of(B - 1), B + 1)


PHASES = 4
INS = dict(x="L0_attn_x", wq="L0_attn_Wq", wk="L0_attn_Wk", wv="L0_attn_Wv", wo="L0_attn_Wo")


def layout(inputs):
    import numpy as np

    a = {k: np.ascontiguousarray(inputs[name]) for k, name in INS.items()}
    columns = lambda *names: np.ascontiguousarray(np.stack([np.reshape(inputs[n], (-1, P)).T for n in names], axis=1))
    a["bqkv"] = columns("L0_attn_bq", "L0_attn_bk", "L0_attn_bv")
    gate, up = (np.transpose(inputs[n], (2, 0, 1)) for n in ("L0_ffn_gate_w", "L0_ffn_up_w"))
    down = np.transpose(np.reshape(inputs["L0_ffn_down_w"], (E0, P, FB0, P)), (3, 0, 2, 1)).reshape(P, E0, FB0 * P)
    a["w0"] = np.ascontiguousarray(np.concatenate([gate, up, down], axis=2).reshape(P, E0 * W0C))
    a["ident"] = np.eye(P, dtype=np.float32)
    r = np.arange(P)
    a["iota"] = np.tile(np.arange(E0, dtype=np.float32), (P, 1))
    hot = np.zeros((HOT_ROWS, E0, P), np.float32)
    hot[np.arange(E0), np.arange(E0)] = hot[LOW + np.arange(E0), np.arange(E0)] = 1
    a["hot"] = hot
    a["zeros"] = np.zeros((P, GT), np.float32)
    for tag, router in (("m0_", np.transpose(inputs["L0_ffn_router_w"])), ("m1_", inputs["L1_ffn_router_w"])):
        a[tag + "rw"] = np.zeros((P, P), np.float32)
        a[tag + "rw"][:, :E0] = router
        a[tag + "rb"] = np.zeros((P, 1), np.float32)
        a[tag + "rb"][:E0, 0] = inputs[f"L{tag[1]}_ffn_router_b"]
    turn = np.zeros((P, P), np.float32)
    half = DH1 // 2
    for m in range(P):
        turn[m + half if m % DH1 < half else m - half, m] = -1 if m % DH1 < half else 1
    a["small"] = np.ascontiguousarray(np.stack([inputs["L1_attn_w_dk"], inputs["L1_attn_w_dv"], turn], axis=1))
    for n in ("w_uk", "w_uv", "w_o", "b_uv"):
        a[n] = np.ascontiguousarray(inputs["L1_attn_" + n])
    a["a1_bias"] = np.ascontiguousarray(np.stack([inputs["L1_attn_" + n] for n in ("b_dk", "b_dv", "b_uk", "b_o")], axis=1))
    inv = np.float32(1) / np.float32(10000) ** (np.arange(0, DH1, 2, dtype=np.float32) / np.float32(DH1))
    angle = np.tile(inv.astype(np.float32), P // half)[:, None] * np.arange(T, dtype=np.float32)[None, :]
    a["cos"], a["sin"] = np.cos(angle), np.sin(angle)
    sel = np.zeros((P, 4, H1 // 4, P), np.float32)
    for f in range(P):
        h, e = f // DH1, f % DH1
        for c in range(4):
            for j, high in ((0, c in (0, 2)), (1, c in (0, 1))):
                sel[f, 2 * j + (0 if high else 1), h // 4, 32 * (h % 4) + 8 * c + e] = 1
    a["sel"] = sel.reshape(P, -1)
    a["in_head"] = (r[:, None] // 32 == np.arange(4)[None, :]).astype(np.float32)
    up = np.transpose(np.concatenate([inputs["L1_ffn_w1"], inputs["L1_ffn_sw1"]]), (1, 0, 2))
    down = np.transpose(np.concatenate([inputs["L1_ffn_w2"], inputs["L1_ffn_sw2"]]).reshape(E1 + S1, FB1, P, P),
                        (2, 0, 1, 3)).reshape(P, E1 + S1, FB1 * P)
    a["w1"] = np.ascontiguousarray(np.concatenate([up, down], axis=2).reshape(P, (E1 + S1) * W1C))
    b1 = np.concatenate([inputs["L1_ffn_b1"], inputs["L1_ffn_sb1"]])
    a["m1_b1"] = np.ascontiguousarray(b1.reshape(-1, P).T)
    a["m1_b2"] = np.zeros((HOT_ROWS, P), np.float32)
    a["m1_b2"][:E1] = a["m1_b2"][LOW:] = inputs["L1_ffn_b2"]
    a["m1_sb2"] = np.ascontiguousarray(inputs["L1_ffn_sb2"].T)
    a["mask"] = np.where(r[None, :] > r[:, None], np.float32(MASKED), np.float32(0))
    return a


def program(nc, d, phases=PHASES):
    with ExitStack() as ctx:
        g = Shared()

        def weights(c, tag, width):
            g.wh = c.enter_context(nc.sbuf_tensor("wh" + tag, [P, width], F32R))
            g.wl = c.enter_context(nc.sbuf_tensor("wl" + tag, [P, width], F32R))

        g.psum = ctx.enter_context(nc.psum_tensor("psum", [P, 8, 512], F32))
        g.spare = ctx.enter_context(nc.sbuf_tensor("spare", [P, 1], F32))
        g.ident = ctx.enter_context(nc.sbuf_tensor("ident", [P, P], F32))
        g.xth = ctx.enter_context(nc.sbuf_tensor("xth", [P, XC], F32R))
        g.xtl = ctx.enter_context(nc.sbuf_tensor("xtl", [P, XC], F32R))
        with ExitStack() as c:
            weights(c, "0", E0 * W0C)
            with ExitStack() as a:
                attention0(nc, a, g, d)
            if phases >= 2:
                moe(nc, c, g, d, "m0_", True)
        if phases >= 3:
            with ExitStack() as c:
                weights(c, "1", (E1 + S1) * W1C)
                with ExitStack() as a:
                    attention1(nc, a, g, d)
                if phases >= 4:
                    moe(nc, c, g, d, "m1_", False)
        if phases < PHASES:
            with nc.semaphore("dbg") as s, nc.Block() as block:
                @block.sync
                def _(sp):
                    sp.dma_start(d["dbg"][0][:, PAD:], g.xth[:, PAD:].bitcast(F32)).then_inc(s, 16)
                    sp.dma_start(d["dbg"][1][:, PAD:], g.xtl[:, PAD:].bitcast(F32)).then_inc(s, 16)
                    sp.wait_ge(s, 32)


def kernel(**inputs):
    import numpy as np
    from concourse import bacc
    from concourse.bass_utils import run_bass_kernel_spmd

    nc = bacc.Bacc("TRN2", target_bir_lowering=False, num_devices=1)
    arrays = layout({name: np.asarray(a) for name, a in inputs.items()})
    d = {k: nc.dram_tensor("in_" + k, a.shape, mybir.dt.from_np(a.dtype), kind="ExternalInput").ap()
         for k, a in arrays.items()}
    d["out"] = nc.dram_tensor("out", (GT + NT, P), F32, kind="ExternalOutput").ap()
    program(nc, d)
    r = run_bass_kernel_spmd(nc, [{"in_" + k: a for k, a in arrays.items()}], core_ids=[0])
    return r.results[0]["out"][GT:].reshape(B, T, P)
```
